# Optimizing a Trainium2 kernel written in Bass

```python
import numpy as np
import jax
import jax.numpy as jnp

def _softmax(x, axis=-1):
    return jax.nn.softmax(x, axis=axis)

def _gelu(x):
    return jax.nn.gelu(x, approximate=True)

def _silu(x):
    return jax.nn.silu(x)

def _sigmoid(x):
    return jax.nn.sigmoid(x)

def _layernorm(x, axis=-1, eps=1e-05):
    m = jnp.mean(x, axis=axis, keepdims=True)
    v = jnp.var(x, axis=axis, keepdims=True)
    return (x - m) / jnp.sqrt(v + eps)

def _scatter_add(tgt, idx, src, axis=0):
    return tgt.at[idx].add(src)

def _segment_sum(src, seg, n):
    return jax.ops.segment_sum(src, seg, n)
kernel_name = 'mk_lm_tower_d1_tok_ids256_r4_f20e33'

def setup_inputs(seed: int=0):
    np.random.seed(seed)
    _w = jnp.asarray

    def _rec_inputs():
        import jax
        import jax.numpy as jnp
        _rk = jax.random.key(seed)
        x = jax.random.randint(jax.random.fold_in(_rk, 1), (4, 512), 0, 12564, jnp.int32)
        return x
    x = _rec_inputs()

    def _L0_tok_setup():
        import jax, jax.numpy as jnp
        import numpy as np
        INP_SIZE = 50257
        HIDDEN = 64
        KSIZE = 9
        B, T = (16, 1024)
        key = jax.random.key(seed)
        k1, k2, k3, k4 = jax.random.split(key, 4)
        x = jax.random.randint(k1, (B, T), 0, INP_SIZE, dtype=jnp.int64 if jax.config.jax_enable_x64 else jnp.int32)
        emb = jax.random.normal(k2, (INP_SIZE, HIDDEN), dtype=jnp.float32) * 0.02
        fan_in = HIDDEN * KSIZE
        bound = 1.0 / np.sqrt(fan_in)
        W = jax.random.uniform(k3, (HIDDEN, HIDDEN, KSIZE), dtype=jnp.float32, minval=-bound, maxval=bound)
        b = jax.random.uniform(k4, (HIDDEN,), dtype=jnp.float32, minval=-bound, maxval=bound)
        return {'x': x, 'emb': emb, 'W': W, 'b': b}
    _L0_tok_all = _L0_tok_setup()
    _L0_tok_in = {k: v for k, v in _L0_tok_all.items() if k in ('emb', 'W', 'b')}
    del _L0_tok_all

    def _L0_attn_setup():
        import jax, jax.numpy as jnp
        import numpy as np
        ALPHA = 0.01
        key = jax.random.key(seed)
        k1, k2, k3 = jax.random.split(key, 3)
        B, N, F_in, F_out = (32, 256, 64, 64)
        inp = jax.random.normal(k1, (B, N, F_in), dtype=jnp.float32)
        lim_W = 1.414 * np.sqrt(6.0 / (F_in + F_out))
        W = jax.random.uniform(k2, (F_in, F_out), dtype=jnp.float32, minval=-lim_W, maxval=lim_W)
        lim_a = 1.414 * np.sqrt(6.0 / (2 * F_out + 1))
        a = jax.random.uniform(k3, (2 * F_out, 1), dtype=jnp.float32, minval=-lim_a, maxval=lim_a)
        return {'inp': inp, 'W': W, 'a': a}
    _L0_attn_all = _L0_attn_setup()
    _L0_attn_in = {k: v for k, v in _L0_attn_all.items() if k in ('W', 'a')}
    del _L0_attn_all

    def _L0_ffn_setup():
        import jax, jax.numpy as jnp
        import numpy as np
        B, S, H, F, E, K = (8, 1024, 64, 128, 16, 2)
        EPS = 1e-05
        key = jax.random.key(seed)
        ks = jax.random.split(key, 9)
        sc = 0.02
        return {'x': jax.random.normal(ks[0], (B, S, H), dtype=jnp.float32), 'gate_w': jax.random.normal(ks[1], (H, E), dtype=jnp.float32) * sc, 'gate_b': jnp.zeros((E,), dtype=jnp.float32), 'w1': jax.random.normal(ks[2], (E, H, F), dtype=jnp.float32) * sc, 'b1': jnp.zeros((E, F), dtype=jnp.float32), 'w2': jax.random.normal(ks[3], (E, F, H), dtype=jnp.float32) * sc, 'b2': jnp.zeros((E, H), dtype=jnp.float32), 'gamma': jnp.ones((H,), dtype=jnp.float32), 'beta': jnp.zeros((H,), dtype=jnp.float32)}
    _L0_ffn_all = _L0_ffn_setup()
    _L0_ffn_in = {k: v for k, v in _L0_ffn_all.items() if k in ('gate_w', 'gate_b', 'w1', 'b1', 'w2', 'b2', 'gamma', 'beta')}
    del _L0_ffn_all
    return {'x': x, 'L0_tok_emb': _L0_tok_in['emb'], 'L0_tok_W': _L0_tok_in['W'], 'L0_tok_b': _L0_tok_in['b'], 'L0_attn_W': _L0_attn_in['W'], 'L0_attn_a': _L0_attn_in['a'], 'L0_ffn_gate_w': _L0_ffn_in['gate_w'], 'L0_ffn_gate_b': _L0_ffn_in['gate_b'], 'L0_ffn_w1': _L0_ffn_in['w1'], 'L0_ffn_b1': _L0_ffn_in['b1'], 'L0_ffn_w2': _L0_ffn_in['w2'], 'L0_ffn_b2': _L0_ffn_in['b2'], 'L0_ffn_gamma': _L0_ffn_in['gamma'], 'L0_ffn_beta': _L0_ffn_in['beta']}

def reference(x, L0_tok_emb, L0_tok_W, L0_tok_b, L0_attn_W, L0_attn_a, L0_ffn_gate_w, L0_ffn_gate_b, L0_ffn_w1, L0_ffn_b1, L0_ffn_w2, L0_ffn_b2, L0_ffn_gamma, L0_ffn_beta):
    import jax
    import jax.numpy as jnp

    def _L0_tok_ref(x, emb, W, b):
        import jax, jax.numpy as jnp
        import numpy as np
        INP_SIZE = 50257
        HIDDEN = 64
        KSIZE = 9
        B, T = (16, 1024)
        offsets = jnp.arange(-(KSIZE // 2), KSIZE // 2 + 1)
        idx = jnp.clip(x[..., None] + offsets, 0, INP_SIZE - 1)
        gathered = emb[idx]
        out = jnp.einsum('btkh,ohk->bto', gathered, W) + b
        return out

    def _L0_attn_ref(inp, W, a):
        import jax, jax.numpy as jnp
        import numpy as np
        ALPHA = 0.01
        h = jnp.matmul(inp, W)
        F_out = W.shape[1]
        a1 = a[:F_out, 0]
        a2 = a[F_out:, 0]
        f1 = jnp.einsum('bnf,f->bn', h, a1)
        f2 = jnp.einsum('bnf,f->bn', h, a2)
        e = f1[:, :, None] + f2[:, None, :]
        e = jnp.where(e > 0, e, ALPHA * e)
        attention = jax.nn.softmax(e, axis=-1)
        h_prime = jnp.matmul(attention, h)
        return jax.nn.elu(h_prime)

    def _L0_ffn_ref(x, gate_w, gate_b, w1, b1, w2, b2, gamma, beta):
        import jax, jax.numpy as jnp
        import numpy as np
        B, S, H, F, E, K = (8, 1024, 64, 128, 16, 2)
        EPS = 1e-05
        gate_logits = x @ gate_w + gate_b
        topk_vals, topk_idx = jax.lax.top_k(gate_logits, K)
        topk_w = jax.nn.softmax(topk_vals, axis=-1)
        h = jax.nn.relu(jnp.einsum('bsh,ehf->bsef', x, w1) + b1)
        expert_out = jnp.einsum('bsef,efh->bseh', h, w2) + b2
        sel = jnp.take_along_axis(expert_out, topk_idx[:, :, :, None], axis=2)
        moe = jnp.sum(topk_w[..., None] * sel, axis=2)
        y = x + moe
        mu = jnp.mean(y, axis=-1, keepdims=True)
        var = jnp.var(y, axis=-1, keepdims=True)
        return (y - mu) / jnp.sqrt(var + EPS) * gamma + beta
    h = _L0_tok_ref(x, L0_tok_emb, L0_tok_W, L0_tok_b)
    h = h + _L0_attn_ref(_layernorm(h, axis=-1), L0_attn_W, L0_attn_a)
    h = h + _L0_ffn_ref(_layernorm(h, axis=-1), L0_ffn_gate_w, L0_ffn_gate_b, L0_ffn_w1, L0_ffn_b1, L0_ffn_w2, L0_ffn_b2, L0_ffn_gamma, L0_ffn_beta)
    return h

_drawn_inputs = setup_inputs


def setup_inputs(seed=0):
    import zlib

    import numpy as np

    out = dict(_drawn_inputs(seed))
    spreads = {'L0_ffn_gate_b': (0.0, 0.1),
     'L0_ffn_b1': (0.0, 0.8),
     'L0_ffn_b2': (0.0, 0.311),
     'L0_ffn_gamma': (1.0, 0.2),
     'L0_ffn_beta': (0.0, 0.1)}
    factors = {'L0_ffn_w1': 7.372, 'L0_ffn_w2': 6.419}
    for name, (base, spread) in spreads.items():
        noise = np.random.default_rng([zlib.crc32(name.encode()), seed]).standard_normal(out[name].shape)
        drawn = base * np.exp(spread * noise) if base else spread * noise
        out[name] = jnp.asarray(drawn.astype(out[name].dtype))
    for name, factor in factors.items():
        out[name] = (out[name] * factor).astype(out[name].dtype)
    return out
```

```python
import concourse.bass as bass
from concourse import mybir
from contextlib import ExitStack

PARTS = 128


def tower(nc, ids, id_row, emb, conv_rows, conv_taps, conv_b, att_w, att_wt, att_a,
          gate_w, gate_b, w1, b1, w2, b2, gamma, beta, out):
    f32, f32r, i32, u32 = mybir.dt.float32, mybir.dt.float32r, mybir.dt.int32, mybir.dt.uint32
    ALU, ACT, AX = mybir.AluOpType, mybir.ActivationFunctionType, mybir.AxisListType.X

    VOCAB, H = emb.shape
    TAPS = conv_taps.shape[1]
    HALF = TAPS // 2
    BATCHES, SEQ, _ = out.shape
    TILES = SEQ // PARTS
    E, F = b1.shape[1], b1.shape[0]
    PAIRS = E // 2
    ADDS = PAIRS - 1
    WIN = TAPS * H
    FULL = WIN // PARTS
    REST = WIN - FULL * PARTS
    EDGE = 4 * HALF
    BIAS_ROW = REST + EDGE
    LAST = BIAS_ROW + 1
    NH = H + 2
    ALPHA, EPS = 0.01, 1e-5
    SLOTS = 2

    ctx = ExitStack()
    with ctx:
        def sb(name, shape, dt=f32):
            return ctx.enter_context(nc.sbuf_tensor(name, shape, dt))

        def sem(name):
            return ctx.enter_context(nc.semaphore(name))

        ident = sb("ident", [PARTS, PARTS])
        minus_half = sb("minus_half", [PARTS, TILES])
        expert_no = sb("expert_no", [PARTS, TILES, E])
        id_cols = sb("id_cols", [PARTS, BATCHES * TILES], i32)
        window_at = sb("window_at", [PARTS, BATCHES * TILES], i32)
        window_now = sb("window_now", [PARTS, TILES], i32)
        id_bc = sb("id_bc", [REST + EDGE, BATCHES * SEQ], i32)
        edge_no = sb("edge_no", [REST + EDGE, 1])
        edge_high = sb("edge_high", [REST + EDGE, 1])
        edge_id = sb("edge_id", [REST + EDGE, 1])
        NV = TAPS + 2 * HALF
        edge_rows = sb("edge_rows", [2 * NV, H])
        edge_rows_t = sb("edge_rows_t", [H, 2 * NV])
        edge_diff = sb("edge_diff", [H, TAPS, EDGE])
        taps = sb("taps", [H, TAPS, H])
        conv_w = sb("conv_w", [PARTS, FULL, H])
        conv_w_last = sb("conv_w_last", [LAST, H])
        att_wt_dup = sb("att_wt_dup", [H, 2, H])
        a_cols = sb("a_cols", [H, 2])
        a_rep = sb("a_rep", [H, 2 + 2 * PARTS])
        wh_raw = sb("wh_raw", [PARTS, NH])
        wh_hi = sb("wh_hi", [PARTS, NH], f32r)
        wh_lo = sb("wh_lo", [H, NH], f32r)
        wf_hi = sb("wf_hi", [PARTS, 2, PARTS], f32r)
        wf_lo = sb("wf_lo", [H, 2, PARTS], f32r)
        gate_raw = sb("gate_raw", [PARTS, E])
        gate_hi = sb("gate_hi", [PARTS, E], f32r)
        gate_lo = sb("gate_lo", [H, E], f32r)
        gate_bias = sb("gate_bias", [PARTS, E])
        w1_raw = sb("w1_raw", [PARTS, E * F])
        w1_hi = sb("w1_hi", [PARTS, E * F], f32r)
        w1_lo = sb("w1_lo", [H, E * F], f32r)
        b1_cols = sb("b1_cols", [F, E])
        w2_sb = sb("w2_sb", [F, E, H])
        b2_sb = sb("b2_sb", [E, H])
        gamma_bc = sb("gamma_bc", [PARTS, H])
        beta_bc = sb("beta_bc", [PARTS, H])

        win = sb("win", [PARTS, TILES, WIN])
        win_t = sb("win_t", [PARTS, TILES, FULL, PARTS])
        win_t_last = sb("win_t_last", [96, SEQ])
        h0 = sb("h0", [PARTS, TILES, H])
        z1 = sb("z1", [PARTS, TILES, 2, H])
        z1_t = sb("z1_t", [PARTS, SEQ], f32r)
        f2_max = sb("f2_max", [PARTS, 1])
        s_min = sb("s_min", [PARTS, SEQ])
        s_max = sb("s_max", [PARTS, SEQ])
        exp_a = sb("exp_a", [PARTS, SEQ])
        exp_b = sb("exp_b", [PARTS, SEQ])
        f2_diff = sb("f2_diff", [PARTS, TILES])
        exp_r = sb("exp_r", [PARTS, TILES])
        hv = sb("hv", [PARTS, TILES, H + 1])
        probs = sb("probs", [PARTS, TILES, SEQ])
        rden = sb("rden", [PARTS, TILES])
        att = sb("att", [PARTS, TILES, H])
        att_neg = sb("att_neg", [PARTS, TILES, H])
        att_exp = sb("att_exp", [PARTS, TILES, H])
        att_res = sb("att_res", [PARTS, TILES, H])
        h1 = sb("h1", [PARTS, TILES, H])
        z2 = sb("z2", [PARTS, TILES, 2, H])
        z2_t = sb("z2_t", [PARTS, SEQ], f32r)
        logits = sb("logits", [PARTS, TILES, E])
        top = sb("top", [PARTS, TILES, 8])
        top_at = sb("top_at", [PARTS, TILES, 8], u32)
        top_no = sb("top_no", [PARTS, TILES, 2])
        gap = sb("gap", [PARTS, TILES])
        gap_exp = sb("gap_exp", [PARTS, TILES])
        gap_sum = sb("gap_sum", [PARTS, TILES])
        gate_1 = sb("gate_1", [PARTS, TILES])
        gate_2 = sb("gate_2", [PARTS, TILES])
        is_1 = sb("is_1", [PARTS, TILES, E])
        is_2 = sb("is_2", [PARTS, TILES, E])
        gates = sb("gates", [PARTS, TILES, E])
        gates_t = sb("gates_t", [E, SEQ])
        ln = [dict(sum=sb(f"ln{n}_sum", [PARTS, TILES]), cen=sb(f"ln{n}_cen", [PARTS, TILES, H]),
                   sqr=sb(f"ln{n}_sqr", [PARTS, TILES, H]), ssq=sb(f"ln{n}_ssq", [PARTS, TILES]),
                   var=sb(f"ln{n}_var", [PARTS, TILES]), rstd=sb(f"ln{n}_rstd", [PARTS, TILES]))
              for n in range(3)]

        hidden = sb("hidden", [F, SLOTS, SEQ])
        scaled = sb("scaled", [PARTS, SLOTS, 2, TILES * H])
        moe = sb("moe", [PARTS, 2, TILES * H])
        y_base = sb("y_base", [PARTS, BATCHES * TILES, H])
        h1_beta = sb("h1_beta", [PARTS, BATCHES * TILES, H])
        moe_sum = sb("moe_sum", [PARTS, TILES, H])
        y = sb("y", [PARTS, TILES, H])
        y_norm = sb("y_norm", [PARTS, TILES, H])
        y_gam = sb("y_gam", [PARTS, TILES, H])
        y_out = sb("y_out", [PARTS, TILES, H])

        bank = [ctx.enter_context(nc.psum_tensor(f"bank{n}", [PARTS, 512], f32)) for n in range(8)]
        ps_a, ps_b, ps_small, ps_wide = bank[0], bank[1], bank[2], bank[7]
        ps_up = bank[3:5]
        ps_down = bank[5:7]
        small_h = ps_small[:, 0:TILES * H].rearrange("p (q h) -> p q h", q=TILES)
        small_nh = ps_small[:, 0:TILES * NH].rearrange("p (q h) -> p q h", q=TILES)
        att_ps = ps_a[:, 0:TILES * (H + 1)].rearrange("p (q h) -> p q h", q=TILES)

        ids_in, rows_in, edge_in, conv_in, att_in, gate_in, w1_in, ffn_in, norm_in = [
            sem(n) for n in ("ids_in", "rows_in", "edge_in", "conv_in", "att_in", "gate_in", "w1_in",
                             "ffn_in", "norm_in")]
        const_made, ident_made, windows_known, edge_known = [
            sem(n) for n in ("const_made", "ident_made", "windows_known", "edge_known")]
        window_copied = sem("window_copied")
        setup_chain = sem("setup_chain")
        edge_rows_ps, edge_rows_sb, edge_diff_sb, edge_ps, conv_w_made = [
            sem(n) for n in ("edge_rows_ps", "edge_rows_sb", "edge_diff_sb", "edge_ps", "conv_w_made")]
        a_rep_made, wa_ps, wa_hi_made, wa_made, gate_hi_made, gate_made, w1_hi_made, w1_made = [
            sem(n) for n in ("a_rep_made", "wa_ps", "wa_hi_made", "wa_made", "gate_hi_made", "gate_made",
                             "w1_hi_made", "w1_made")]
        gathered = [sem(f"gathered{q}") for q in range(TILES)]
        win_t_ps, win_t_act, win_t_dve, win_t_rest, edge_hot, conv_ps = [
            sem(n) for n in ("win_t_ps", "win_t_act", "win_t_dve", "win_t_rest", "edge_hot", "conv_ps")]
        h0_saved, z1_made, z1_t_ps, z1_hi_made, z1_t_made, f2_ps, f1_ps, h_ps = [
            sem(n) for n in ("h0_saved", "z1_made", "z1_t_ps", "z1_hi_made", "z1_t_made", "f2_ps", "f1_ps",
                             "h_ps")]
        s_min_made, s_max_made, f2_diff_made, exp_a_made, exp_b_made, exp_r_made, exp_v_made = [
            sem(n) for n in ("s_min_made", "s_max_made", "f2_diff_made", "exp_a_made", "exp_b_made",
                             "exp_r_made", "exp_v_made")]
        probs_made, hv_made, att_done, att_neg_made, att_exp_made, h1_made, h1_beta_made = [
            sem(n) for n in ("probs_made", "hv_made", "att_done", "att_neg_made", "att_exp_made", "h1_made",
                             "h1_beta_made")]
        z2_made, z2_t_ps, z2_hi_made, z2_t_made, logits_ps, gap_made, gap_exp_made, gates_made = [
            sem(n) for n in ("z2_made", "z2_t_ps", "z2_hi_made", "z2_t_made", "logits_ps", "gap_made",
                             "gap_exp_made", "gates_made")]
        var_made = [sem(f"var_made{n}") for n in range(3)]
        rstd_made = [sem(f"rstd_made{n}") for n in range(3)]
        gates_t_ps, gates_t_made, b2_ps, y_base_made = [
            sem(n) for n in ("gates_t_ps", "gates_t_made", "b2_ps", "y_base_made")]
        up_ps, hidden_made, down_ps, scaled_made, moe_added, moe_read, out_made, out_stored = [
            sem(n) for n in ("up_ps", "hidden_made", "down_ps", "scaled_made", "moe_added", "moe_read",
                             "out_made", "out_stored")]
        logits_made = sem("logits_made")
        front_chain, ffn_chain = sem("front_chain"), sem("ffn_chain")

        block = ctx.enter_context(nc.Block())

        def tiles(t, b):
            return t[:, bass.ds(b * TILES, TILES), :]

        def over_h(t, n=H):
            return t.unsqueeze(2).to_broadcast([PARTS, TILES, n])

        @block.sync
        def _(sp):
            sp.dma_start(id_cols[:, :], ids).then_inc(ids_in, 16)
            sp.dma_start(id_bc[REST:REST + EDGE, :], id_row.to_broadcast([EDGE, BATCHES * SEQ])).then_inc(rows_in, 16)
            sp.dma_start(taps[:, :, :], conv_taps).then_inc(edge_in, 16)
            sp.dma_start(conv_w[:, :, :], conv_rows[0:FULL * PARTS, :].rearrange("(c p) o -> p c o", p=PARTS)).then_inc(conv_in, 16)
            sp.dma_start(conv_w_last[0:REST, :], conv_rows[FULL * PARTS:WIN, :]).then_inc(conv_in, 16)
            sp.dma_start(conv_w_last[BIAS_ROW:LAST, :], conv_b).then_inc(conv_in, 16)
            sp.dma_start(w1_raw[0:H, :], w1).then_inc(w1_in, 16)
            sp.dma_start(w1_raw[H:2 * H, :], w1).then_inc(w1_in, 16)
            sp.dma_start(w2_sb[:, :, :], w2).then_inc(ffn_in, 16)
            sp.dma_start(b1_cols[:, :], b1).then_inc(ffn_in, 16)
            sp.dma_start(b2_sb[:, :], b2).then_inc(ffn_in, 16)
            sp.dma_start(beta_bc[:, :], beta.to_broadcast([PARTS, H])).then_inc(norm_in, 16)
            sp.dma_start(gamma_bc[:, :], gamma.to_broadcast([PARTS, H])).then_inc(norm_in, 16)
            sp.sem_inc(out_stored, 1)
            with sp.Fori(0, BATCHES) as b:
                sp.wait_ge(out_made, b + 1)
                sp.dma_start(out[bass.ds(b, 1), :, :].rearrange("a (p q) h -> p (a q h)", q=TILES),
                             y_out[:, :, :].rearrange("p q h -> p (q h)")).then_inc(out_stored, 16)
            sp.wait_ge(out_stored, 16 * BATCHES + 1)

        @block.gpsimd
        def _(pool):
            pool.memset(ident[:, :], 0.0).then_inc(ident_made, 1)
            pool.memset(minus_half[:, :], -0.5).then_inc(const_made, 1)
            pool.wait_ge(ident_made, 1)
            pool.affine_select(out=ident[:, :], in_=ident[:, :], compare_op=ALU.not_equal, fill=1.0, base=0,
                               pattern=[[-1, PARTS]], channel_multiplier=1).then_inc(ident_made, 1)
            pool.wait_ge(ident_made, 2)
            pool.iota(edge_no[REST:REST + EDGE, :], pattern=[[0, 1]], base=0, channel_multiplier=1,
                      allow_small_or_imprecise_dtypes=True).then_inc(const_made, 1)

            def gather(b, q):
                pool.indirect_dma_start(win[:, q, :], None, emb,
                                        bass.IndirectOffsetOnAxis(ap=window_at[:, b * TILES + q:b * TILES + q + 1], axis=0)
                                        ).then_inc(gathered[q], 16)

            def gather_next(b):
                for q in range(TILES):
                    pool.wait_ge(windows_known, 2)
                    pool.wait_ge(win_t_ps, b * TILES + q + 1)
                    pool.tensor_copy(window_now[:, q:q + 1], window_at[:, bass.ds((b + 1) * TILES + q, 1)]).then_inc(window_copied, 1)
                    pool.wait_ge(windows_known, 2)
                    pool.wait_ge(window_copied, b * TILES + q + 1)
                    pool.indirect_dma_start(win[:, q, :], None, emb,
                                            bass.IndirectOffsetOnAxis(ap=window_now[:, q:q + 1], axis=0)
                                            ).then_inc(gathered[q], 16)

            def inverse_deviation(n, b):
                pool.wait_ge(var_made[n], b + 1)
                pool.tensor_tensor(ln[n]["rstd"][:, :], ln[n]["var"][:, :], minus_half[:, :], ALU.pow).then_inc(rstd_made[n], 1)

            def add_pair(b, pair):
                pool.wait_ge(scaled_made, b * PAIRS + pair + 1 + SLOTS)
                now = scaled[:, pair % SLOTS, :, :]
                if pair == 1:
                    pool.wait_ge(moe_read, b + 1)
                    pool.tensor_tensor(moe[:, :, :], scaled[:, 0, :, :], now, ALU.add).then_inc(moe_added, 1)
                else:
                    pool.wait_ge(moe_added, b * ADDS + pair)
                    pool.tensor_tensor(moe[:, :, :], moe[:, :, :], now, ALU.add).then_inc(moe_added, 1)

            def add_beta(b):
                pool.wait_ge(h1_made, b + 1)
                pool.tensor_tensor(tiles(h1_beta, b), h1[:, :, :],
                                   beta_bc[:, :].unsqueeze(1).to_broadcast([PARTS, TILES, H]), ALU.add).then_inc(h1_beta_made, 1)

            def iteration(front, ffn, last):
                if front is not None and not last:
                    gather_next(front)
                if ffn is not None:
                    add_pair(ffn, 1)
                    add_pair(ffn, 2)
                if front is not None:
                    inverse_deviation(0, front)
                if ffn is not None:
                    for pair in range(3, 7):
                        add_pair(ffn, pair)
                if front is not None:
                    add_beta(front)
                    inverse_deviation(1, front)
                if ffn is not None:
                    add_pair(ffn, 7)
                    inverse_deviation(2, ffn)

            pool.wait_ge(windows_known, 2)
            for q in range(TILES):
                gather(0, q)
            pool.wait_ge(const_made, 2)
            pool.wait_ge(norm_in, 32)
            pool.sem_inc(moe_added, 1)
            iteration(0, None, False)
            with pool.Fori(1, BATCHES - 1) as b:
                iteration(b, b - 1, False)
            iteration(BATCHES - 1, BATCHES - 2, True)
            iteration(None, BATCHES - 1, True)

        @block.scalar
        def _(act):
            act.dma_start(edge_rows[0:2 * HALF, :], emb[0:1, :].to_broadcast([2 * HALF, H])).then_inc(edge_in, 16)
            act.dma_start(edge_rows[2 * HALF:NV, :], emb[0:TAPS, :]).then_inc(edge_in, 16)
            act.dma_start(edge_rows[NV:NV + TAPS, :], emb[VOCAB - TAPS:VOCAB, :]).then_inc(edge_in, 16)
            act.dma_start(edge_rows[NV + TAPS:2 * NV, :], emb[VOCAB - 1:VOCAB, :].to_broadcast([2 * HALF, H])).then_inc(edge_in, 16)
            act.dma_start(a_cols[:, :], att_a).then_inc(att_in, 16)
            act.dma_start(att_wt_dup[:, 0, :], att_wt).then_inc(att_in, 16)
            act.dma_start(att_wt_dup[:, 1, :], att_wt).then_inc(att_in, 16)
            act.dma_start(wh_raw[0:H, 0:H], att_w).then_inc(att_in, 16)
            act.dma_start(wh_raw[H:2 * H, 0:H], att_w).then_inc(att_in, 16)
            act.dma_start(gate_raw[0:H, :], gate_w).then_inc(gate_in, 16)
            act.dma_start(gate_raw[H:2 * H, :], gate_w).then_inc(gate_in, 16)
            act.dma_start(gate_bias[:, :], gate_b.to_broadcast([PARTS, E])).then_inc(gate_in, 16)

            act.wait_ge(edge_rows_ps, 1)
            act.activation(edge_rows_t[:, :], ps_up[0][0:H, 0:2 * NV], ACT.Copy).then_inc(edge_rows_sb, 1)
            act.wait_ge(wa_ps, 1)
            act.activation(wh_raw[:, H:NH], ps_down[0][:, 0:2], ACT.Copy).then_inc(wa_hi_made, 1)
            act.activation(wf_hi[:, :, :].rearrange("p a b -> p (a b)"), ps_down[0][:, 2:2 + 2 * PARTS], ACT.Copy).then_inc(wa_hi_made, 1)
            act.wait_ge(att_in, 16 * 5)
            act.wait_ge(wa_hi_made, 2)
            act.activation(wh_hi[:, :], wh_raw[:, :], ACT.Copy).then_inc(wa_hi_made, 1)
            act.wait_ge(gate_in, 16 * 3)
            act.activation(gate_hi[:, :], gate_raw[:, :], ACT.Copy).then_inc(gate_hi_made, 1)

            def copy_windows(b, q):
                act.wait_ge(win_t_ps, b * TILES + q + 1)
                act.activation(win_t[:, q, :, :].rearrange("p c t -> p (c t)"), bank[q % 2][:, :], ACT.Copy).then_inc(win_t_act, 1)

            def copy_last_rows(b):
                act.wait_ge(win_t_ps, b * TILES + TILES)
                act.activation(win_t_last[0:REST, :], ps_wide[0:REST, :], ACT.Copy).then_inc(win_t_rest, 1)

            def save_h0(b):
                act.wait_ge(conv_ps, b + 1)
                act.activation(h0[:, :, :], small_h, ACT.Copy).then_inc(h0_saved, 1)

            def round_z1(b):
                act.wait_ge(z1_t_ps, b + 1)
                act.activation(z1_t[:, :], ps_a[:, :], ACT.Copy).then_inc(z1_hi_made, 1)

            def exps(b):
                act.wait_ge(s_min_made, b + 1)
                act.activation(exp_a[:, :], s_min[:, :], ACT.Exp, scale=1.0 - ALPHA).then_inc(exp_a_made, 1)
                act.wait_ge(f2_diff_made, b + 1)
                act.activation(exp_r[:, :], f2_diff[:, :], ACT.Exp, scale=1.0 - ALPHA).then_inc(exp_r_made, 1)
                act.activation(hv[:, :, H:H + 1], f2_diff[:, :].unsqueeze(2), ACT.Exp, scale=ALPHA).then_inc(exp_v_made, 1)
                act.wait_ge(s_max_made, b + 1)
                act.activation(exp_b[:, :], s_max[:, :], ACT.Exp, scale=-(1.0 - ALPHA)).then_inc(exp_b_made, 1)

            def exp_negative_part(b):
                act.wait_ge(att_neg_made, b + 1)
                act.activation(att_exp[:, :, :], att_neg[:, :, :], ACT.Exp).then_inc(att_exp_made, 1)

            def round_z2(b):
                act.wait_ge(z2_t_ps, b + 1)
                act.activation(z2_t[:, :], ps_b[:, :], ACT.Copy).then_inc(z2_hi_made, 1)

            def exp_gap(b):
                act.wait_ge(gap_made, b + 1)
                act.activation(gap_exp[:, :], gap[:, :], ACT.Exp).then_inc(gap_exp_made, 1)

            def copy_gates_t(b):
                act.wait_ge(gates_t_ps, b + 1)
                act.activation(gates_t[:, :], ps_wide[0:E, :], ACT.Copy).then_inc(gates_t_made, 1)

            def hide(b, pair):
                for e in (2 * pair, 2 * pair + 1):
                    act.wait_ge(up_ps, b * E + e + 1)
                    act.wait_ge(down_ps, b * E + e + 1)
                    act.activation(hidden[:, e % SLOTS, :], ps_up[e % SLOTS][:, :], ACT.Relu,
                                   bias=b1_cols[:, e:e + 1]).then_inc(hidden_made, 1)

            def iteration(front, ffn):
                if ffn is not None:
                    hide(ffn, 0)
                    copy_gates_t(ffn)
                if front is not None:
                    copy_windows(front, 0)
                    copy_windows(front, 2)
                    copy_last_rows(front)
                if ffn is not None:
                    hide(ffn, 1)
                if front is not None:
                    save_h0(front)
                if ffn is not None:
                    hide(ffn, 2)
                    hide(ffn, 3)
                if front is not None:
                    round_z1(front)
                if ffn is not None:
                    hide(ffn, 4)
                if front is not None:
                    exps(front)
                if ffn is not None:
                    hide(ffn, 5)
                if front is not None:
                    exp_negative_part(front)
                if ffn is not None:
                    hide(ffn, 6)
                    hide(ffn, 7)
                if front is not None:
                    round_z2(front)
                    exp_gap(front)

            iteration(0, None)
            act.wait_ge(w1_in, 32)
            act.activation(w1_hi[:, :], w1_raw[:, :], ACT.Copy).then_inc(w1_hi_made, 1)
            act.wait_ge(ffn_in, 48)
            act.sem_inc(hidden_made, SLOTS)
            with act.Fori(1, BATCHES) as b:
                iteration(b, b - 1)
            iteration(None, BATCHES - 1)

        @block.tensor
        def _(pe):
            def split_matmul(dst, lhs, lhs_lo, rhs, rhs_lo):
                nc.tensor.matmul(dst, lhs, rhs, start=True, stop=False)
                return nc.tensor.matmul(dst, lhs_lo, rhs_lo, start=False, stop=True)

            pe.sem_inc(down_ps, SLOTS)
            pe.wait_ge(ident_made, 2)
            pe.wait_ge(edge_in, 16 * 5)
            nc.tensor.transpose(ps_up[0][0:H, 0:2 * NV], edge_rows[:, :], ident[0:2 * NV, 0:2 * NV]).then_inc(edge_rows_ps, 1)
            pe.wait_ge(a_rep_made, 3)
            nc.tensor.matmul(ps_down[0][:, 0:2 + 2 * PARTS], att_wt_dup[:, :, :].rearrange("f a h -> f (a h)"), a_rep[:, :],
                             start=True, stop=True).then_inc(wa_ps, 1)
            pe.wait_ge(edge_diff_sb, 1)
            for k in range(TAPS):
                last = nc.tensor.matmul(ps_up[1][REST:REST + EDGE, 0:H], edge_diff[:, k, :], taps[:, k, :],
                                        start=(k == 0), stop=(k == TAPS - 1))
            last.then_inc(edge_ps, 1)

            def turn_windows(b):
                for q in range(TILES):
                    pe.wait_ge(gathered[q], 16 * (b + 1))
                    if q == 0:
                        pe.wait_ge(h1_made, b)
                        pe.wait_ge(gates_t_made, b)
                    elif q == 1:
                        pe.wait_ge(z2_t_made, b)
                    elif q == 2:
                        pe.wait_ge(win_t_act, 2 * b + 1)
                    else:
                        pe.wait_ge(win_t_dve, 2 * b + 1)
                    for c in range(FULL):
                        nc.tensor.transpose(bank[q % 2][:, c * PARTS:(c + 1) * PARTS],
                                            win[:, q, c * PARTS:(c + 1) * PARTS], ident[:, :])
                    nc.tensor.transpose(ps_wide[0:REST, q * PARTS:(q + 1) * PARTS],
                                        win[:, q, FULL * PARTS:WIN], ident[:, :]).then_inc(win_t_ps, 1)

            def convolve(b):
                pe.wait_ge(win_t_act, 2 * b + 2)
                pe.wait_ge(win_t_dve, 2 * b + 2)
                pe.wait_ge(win_t_rest, b + 1)
                pe.wait_ge(edge_hot, b + 1)
                pe.wait_ge(y_base_made, b)
                for q in range(TILES):
                    for c in range(FULL):
                        nc.tensor.matmul(small_h[:, q, :], win_t[:, q, c, :], conv_w[:, c, :], start=(c == 0), stop=False)
                    last = nc.tensor.matmul(small_h[:, q, :], win_t_last[0:LAST, q * PARTS:(q + 1) * PARTS],
                                            conv_w_last[:, :], start=False, stop=True)
                last.then_inc(conv_ps, 1)

            def turn_z1(b):
                pe.wait_ge(z1_made, b + 1)
                for q in range(TILES):
                    last = nc.tensor.transpose(ps_a[:, q * PARTS:(q + 1) * PARTS],
                                               z1[:, q, :, :].rearrange("p a h -> p (a h)"), ident[:, :])
                last.then_inc(z1_t_ps, 1)

            def project(b):
                pe.wait_ge(z1_t_made, b + 1)
                split_matmul(ps_wide[:, :], wf_hi[:, 1, :], wf_lo[:, 1, :], z1_t[:, :], z1_t[0:H, :]).then_inc(f2_ps, 1)
                split_matmul(ps_b[:, :], wf_hi[:, 0, :], wf_lo[:, 0, :], z1_t[:, :], z1_t[0:H, :]).then_inc(f1_ps, 1)
                pe.wait_ge(h0_saved, b + 1)
                for q in range(TILES):
                    cols = slice(q * PARTS, (q + 1) * PARTS)
                    last = split_matmul(small_nh[:, q, :], z1_t[:, cols], z1_t[0:H, cols], wh_hi[:, :], wh_lo[:, :])
                last.then_inc(h_ps, 1)

            def attend(b):
                pe.wait_ge(probs_made, b + 1)
                pe.wait_ge(hv_made, b + 1)
                for i in range(TILES):
                    for j in range(TILES):
                        last = nc.tensor.matmul(att_ps[:, i, :], probs[:, j, i * PARTS:(i + 1) * PARTS], hv[:, j, :],
                                                start=(j == 0), stop=(j == TILES - 1))
                last.then_inc(att_done, 1)

            def turn_z2(b):
                pe.wait_ge(z2_made, b + 1)
                for q in range(TILES):
                    last = nc.tensor.transpose(ps_b[:, q * PARTS:(q + 1) * PARTS],
                                               z2[:, q, :, :].rearrange("p a h -> p (a h)"), ident[:, :])
                last.then_inc(z2_t_ps, 1)

            def gate(b):
                pe.wait_ge(z2_t_made, b + 1)
                for q in range(TILES):
                    cols = slice(q * PARTS, (q + 1) * PARTS)
                    last = split_matmul(ps_wide[:, q * E:(q + 1) * E], z2_t[:, cols], z2_t[0:H, cols], gate_hi[:, :], gate_lo[:, :])
                last.then_inc(logits_ps, 1)

            def expert_bias(b):
                pe.wait_ge(gates_made, b + 1)
                for q in range(TILES):
                    last = nc.tensor.transpose(ps_wide[0:E, q * PARTS:(q + 1) * PARTS], gates[:, q, :], ident[:, :])
                last.then_inc(gates_t_ps, 1)
                pe.wait_ge(gates_t_made, b + 1)
                for q in range(TILES):
                    last = nc.tensor.matmul(small_h[:, q, :], gates_t[:, q * PARTS:(q + 1) * PARTS], b2_sb[:, :], start=True, stop=True)
                last.then_inc(b2_ps, 1)

            def up(b, e):
                pe.wait_ge(hidden_made, b * E + e + 1)
                split_matmul(ps_up[e % SLOTS][:, :], w1_hi[:, e * F:(e + 1) * F], w1_lo[:, e * F:(e + 1) * F],
                             z2_t[:, :], z2_t[0:H, :]).then_inc(up_ps, 1)

            def experts(b, pair):
                down = ps_down[pair % SLOTS][:, :].rearrange("p (a q h) -> p a q h", a=2, q=TILES)
                for e in (2 * pair, 2 * pair + 1):
                    up(b, e)
                pe.wait_ge(scaled_made, b * PAIRS + pair + 1)
                for e in (2 * pair, 2 * pair + 1):
                    pe.wait_ge(hidden_made, b * E + e + 1 + SLOTS)
                    for q in range(TILES):
                        last = nc.tensor.matmul(down[:, e % 2, q, :], hidden[:, e % SLOTS, q * PARTS:(q + 1) * PARTS],
                                                w2_sb[:, e, :], start=True, stop=True)
                    last.then_inc(down_ps, 1)

            def iteration(front, ffn):
                if ffn is not None:
                    experts(ffn, 0)
                    expert_bias(ffn)
                if front is not None:
                    turn_windows(front)
                if ffn is not None:
                    experts(ffn, 1)
                if front is not None:
                    if ffn is None:
                        pe.wait_ge(conv_in, 48)
                        pe.wait_ge(conv_w_made, 1)
                    convolve(front)
                if ffn is not None:
                    experts(ffn, 2)
                    experts(ffn, 3)
                if front is not None:
                    turn_z1(front)
                if ffn is not None:
                    experts(ffn, 4)
                if front is not None:
                    if ffn is None:
                        pe.wait_ge(wa_hi_made, 3)
                        pe.wait_ge(wa_made, 2)
                    project(front)
                if ffn is not None:
                    experts(ffn, 5)
                if front is not None:
                    attend(front)
                if ffn is not None:
                    experts(ffn, 6)
                    experts(ffn, 7)
                if front is not None:
                    turn_z2(front)
                    if ffn is None:
                        pe.wait_ge(gate_hi_made, 1)
                        pe.wait_ge(gate_made, 1)
                    gate(front)

            iteration(0, None)
            pe.wait_ge(w1_hi_made, 1)
            pe.wait_ge(w1_made, 1)
            pe.wait_ge(ffn_in, 48)
            with pe.Fori(1, BATCHES) as b:
                iteration(b, b - 1)
            iteration(None, BATCHES - 1)

        @block.vector
        def _(dve):
            done = [0]

            def linked(ins):
                done[0] += 1
                ins.then_inc(setup_chain, 1)
                dve.wait_ge(setup_chain, done[0])

            dve.wait_ge(ids_in, 16)
            linked(nc.vector.tensor_scalar(window_at[:, :], id_cols[:, :], float(HALF), 0.0, ALU.subtract, ALU.max))
            nc.vector.tensor_scalar(window_at[:, :], window_at[:, :], float(VOCAB - TAPS), None, ALU.min).then_inc(windows_known, 2)
            nc.vector.memset(win_t_last[REST:96, :], 1.0).then_inc(setup_chain, 1)
            done[0] += 1
            dve.wait_ge(att_in, 16 * 5)
            nc.vector.tensor_copy(a_rep[:, 0:2], a_cols[:, 1:2].to_broadcast([H, 2])).then_inc(a_rep_made, 1)
            nc.vector.tensor_copy(a_rep[:, 2:2 + PARTS], a_cols[:, 0:1].to_broadcast([H, PARTS])).then_inc(a_rep_made, 1)
            nc.vector.tensor_copy(a_rep[:, 2 + PARTS:], a_cols[:, 1:2].to_broadcast([H, PARTS])).then_inc(a_rep_made, 1)
            dve.wait_ge(const_made, 2)
            edge = slice(REST, REST + EDGE)
            linked(nc.vector.tensor_scalar(edge_high[edge, :], edge_no[edge, :], 2.0 * HALF - 0.5, float(VOCAB - 2 * HALF),
                                           ALU.is_gt, ALU.mult))
            linked(nc.vector.scalar_tensor_tensor(edge_id[edge, :], edge_no[edge, :], float(-HALF), edge_high[edge, :], ALU.add, ALU.add))
            dve.wait_ge(rows_in, 16)
            linked(nc.vector.tensor_scalar(id_bc[edge, :], id_bc[edge, :], float(-HALF), float(VOCAB + HALF - 1), ALU.max, ALU.min))
            dve.wait_ge(edge_rows_sb, 1)
            for k in range(TAPS):
                for end, first, base in ((0, k, 2 * HALF + k), (1, NV + 1 + k, NV + k)):
                    last = nc.vector.tensor_scalar(edge_diff[:, k, end * 2 * HALF:(end + 1) * 2 * HALF],
                                                   edge_rows_t[:, first:first + 2 * HALF], edge_rows_t[:, base:base + 1],
                                                   None, ALU.subtract)
                    linked(last)
            nc.vector.memset(moe_sum[:, 0:1, 0:1], 0.0).then_inc(edge_diff_sb, 1)
            dve.wait_ge(edge_ps, 1)
            nc.vector.tensor_copy(conv_w_last[edge, :], ps_up[1][edge, 0:H]).then_inc(conv_w_made, 1)
            dve.wait_ge(wa_hi_made, 3)
            nc.vector.tensor_tensor(wh_lo[:, :], wh_raw[0:H, :], wh_hi[0:H, :].bitcast(f32), ALU.subtract).then_inc(wa_made, 1)
            nc.vector.tensor_tensor(wf_lo[:, :, :].rearrange("p a b -> p (a b)"), ps_down[0][0:H, 2:2 + 2 * PARTS],
                                    wf_hi[0:H, :, :].rearrange("p a b -> p (a b)").bitcast(f32), ALU.subtract).then_inc(wa_made, 1)
            dve.wait_ge(gate_hi_made, 1)
            nc.vector.tensor_tensor(gate_lo[:, :], gate_raw[0:H, :], gate_hi[0:H, :].bitcast(f32), ALU.subtract).then_inc(gate_made, 1)
            for e in range(E):
                last = nc.vector.memset(expert_no[:, :, e:e + 1], float(e))
                linked(last)

            FRONT_LINKS, FFN_LINKS = 22, 7
            count = {}

            def link(ins, b, chain, per):
                count[chain] = count.get(chain, 0) + 1
                ins.then_inc(chain, 1)
                dve.wait_ge(chain, b * per + count[chain])

            def f_link(ins, b):
                link(ins, b, front_chain, FRONT_LINKS)

            def e_link(ins, b):
                link(ins, b, ffn_chain, FFN_LINKS)

            def normalise(n, b, src, linker):
                t = ln[n]
                linker(nc.vector.tensor_reduce(t["sum"][:, :], src, axis=AX, op=ALU.add), b)
                linker(nc.vector.scalar_tensor_tensor(t["cen"][:, :, :], over_h(t["sum"][:, :]), -1.0 / H, src, ALU.mult, ALU.add), b)
                linker(nc.vector.tensor_tensor(t["sqr"][:, :, :], t["cen"][:, :, :], t["cen"][:, :, :], ALU.mult), b)
                linker(nc.vector.tensor_reduce(t["ssq"][:, :], t["sqr"][:, :, :], axis=AX, op=ALU.add), b)
                nc.vector.tensor_scalar(t["var"][:, :], t["ssq"][:, :], 1.0 / H, EPS, ALU.mult, ALU.add).then_inc(var_made[n], 1)

            def scale_twice(n, b, dst):
                dve.wait_ge(rstd_made[n], b + 1)
                return nc.vector.tensor_tensor(dst, ln[n]["cen"][:, :, :].unsqueeze(2).to_broadcast([PARTS, TILES, 2, H]),
                                               ln[n]["rstd"][:, :].unsqueeze(2).unsqueeze(3).to_broadcast([PARTS, TILES, 2, H]),
                                               ALU.mult)

            def copy_windows(b, q):
                dve.wait_ge(win_t_ps, b * TILES + q + 1)
                nc.vector.tensor_copy(win_t[:, q, :, :].rearrange("p c t -> p (c t)"), bank[q % 2][:, :]).then_inc(win_t_dve, 1)

            def mark_edges(b):
                dve.wait_ge(conv_ps, b)
                nc.vector.tensor_scalar(win_t_last[edge, :], id_bc[edge, bass.ds(b * SEQ, SEQ)], edge_id[edge, :], None,
                                        ALU.is_equal).then_inc(edge_hot, 1)

            def norm_h0(b):
                dve.wait_ge(h0_saved, b + 1)
                normalise(0, b, h0[:, :, :], f_link)

            def make_z1(b):
                scale_twice(0, b, z1[:, :, :, :]).then_inc(z1_made, 1)

            def split_z1(b):
                dve.wait_ge(z1_hi_made, b + 1)
                nc.vector.tensor_tensor(z1_t[H:2 * H, :], ps_a[H:2 * H, :], z1_t[H:2 * H, :].bitcast(f32), ALU.subtract).then_inc(z1_t_made, 1)

            def scores(b):
                dve.wait_ge(f2_ps, b + 1)
                f_link(nc.vector.tensor_reduce(f2_max[:, :], ps_wide[:, :], axis=AX, op=ALU.max), b)
                dve.wait_ge(f1_ps, b + 1)
                nc.vector.tensor_scalar(s_min[:, :], ps_b[:, :], f2_max[:, :], 0.0, ALU.add, ALU.min).then_inc(s_min_made, 1)
                dve.wait_ge(h_ps, b + 1)
                nc.vector.tensor_scalar(f2_diff[:, :].unsqueeze(2), small_nh[:, :, H:H + 1], f2_max[:, :], None, ALU.subtract).then_inc(f2_diff_made, 1)
                nc.vector.tensor_scalar(s_max[:, :], ps_b[:, :], f2_max[:, :], 0.0, ALU.add, ALU.max).then_inc(s_max_made, 1)

            def make_probs(b):
                dve.wait_ge(exp_v_made, b + 1)
                nc.vector.tensor_tensor(hv[:, :, 0:H], small_nh[:, :, 0:H], hv[:, :, H:H + 1].to_broadcast([PARTS, TILES, H]),
                                        ALU.mult).then_inc(hv_made, 1)
                dve.wait_ge(exp_a_made, b + 1)
                dve.wait_ge(exp_r_made, b + 1)
                dve.wait_ge(exp_b_made, b + 1)
                for j in range(TILES):
                    last = nc.vector.scalar_tensor_tensor(probs[:, j, :], exp_a[:, :], exp_r[:, j:j + 1], exp_b[:, :], ALU.mult, ALU.max)
                last.then_inc(probs_made, 1)

            def finish_attention(b):
                dve.wait_ge(att_done, b + 1)
                f_link(nc.vector.reciprocal(rden[:, :].unsqueeze(2), att_ps[:, :, H:H + 1]), b)
                f_link(nc.vector.tensor_tensor(att[:, :, :], att_ps[:, :, 0:H], over_h(rden[:, :]), ALU.mult), b)
                nc.vector.tensor_scalar(att_neg[:, :, :], att[:, :, :], 0.0, None, ALU.min).then_inc(att_neg_made, 1)
                dve.wait_ge(h0_saved, b + 1)
                f_link(nc.vector.scalar_tensor_tensor(att_res[:, :, :], att[:, :, :], 0.0, h0[:, :, :], ALU.max, ALU.add), b)
                dve.wait_ge(att_exp_made, b + 1)
                dve.wait_ge(h1_beta_made, b)
                nc.vector.scalar_tensor_tensor(h1[:, :, :], att_exp[:, :, :], -1.0, att_res[:, :, :], ALU.add, ALU.add).then_inc(h1_made, 1)
                dve.wait_ge(h1_made, b + 1)
                normalise(1, b, h1[:, :, :], f_link)

            def make_z2(b):
                scale_twice(1, b, z2[:, :, :, :]).then_inc(z2_made, 1)

            def split_z2(b):
                dve.wait_ge(z2_hi_made, b + 1)
                nc.vector.tensor_tensor(z2_t[H:2 * H, :], ps_b[H:2 * H, :], z2_t[H:2 * H, :].bitcast(f32), ALU.subtract).then_inc(z2_t_made, 1)

            def choose_experts(b):
                dve.wait_ge(logits_ps, b + 1)
                nc.vector.tensor_tensor(logits[:, :, :], ps_wide[:, 0:TILES * E].rearrange("p (q e) -> p q e", q=TILES),
                                        gate_bias[:, :].unsqueeze(1).to_broadcast([PARTS, TILES, E]), ALU.add).then_inc(logits_made, 1)
                dve.wait_ge(windows_known, 2)
                dve.wait_ge(logits_made, b + 1)
                for q in range(TILES):
                    last = nc.vector.max(top[:, q, :], logits[:, q, :])
                f_link(last, b)
                nc.vector.tensor_tensor(gap[:, :].unsqueeze(2), top[:, :, 1:2], top[:, :, 0:1], ALU.subtract).then_inc(gap_made, 1)
                for q in range(TILES):
                    last = nc.vector.max_index(top_at[:, q, :], top[:, q, :], logits[:, q, :])
                f_link(last, b)
                f_link(nc.vector.tensor_copy(top_no[:, :, :], top_at[:, :, 0:2]), b)
                f_link(nc.vector.tensor_tensor(is_1[:, :, :], expert_no[:, :, :], top_no[:, :, 0:1].to_broadcast([PARTS, TILES, E]), ALU.is_equal), b)
                f_link(nc.vector.tensor_tensor(is_2[:, :, :], expert_no[:, :, :], top_no[:, :, 1:2].to_broadcast([PARTS, TILES, E]), ALU.is_equal), b)
                dve.wait_ge(gap_exp_made, b + 1)
                f_link(nc.vector.tensor_scalar(gap_sum[:, :], gap_exp[:, :], 1.0, None, ALU.add), b)
                f_link(nc.vector.reciprocal(gate_1[:, :], gap_sum[:, :]), b)
                f_link(nc.vector.tensor_tensor(gate_2[:, :], gap_exp[:, :], gate_1[:, :], ALU.mult), b)
                f_link(nc.vector.tensor_tensor(is_1[:, :, :], is_1[:, :, :], over_h(gate_1[:, :], E), ALU.mult), b)
                f_link(nc.vector.tensor_tensor(is_2[:, :, :], is_2[:, :, :], over_h(gate_2[:, :], E), ALU.mult), b)
                nc.vector.tensor_tensor(gates[:, :, :], is_1[:, :, :], is_2[:, :, :], ALU.add).then_inc(gates_made, 1)

            def scale_pair(b, pair):
                dve.wait_ge(down_ps, b * E + 2 * pair + 2 + SLOTS)
                dve.wait_ge(moe_added, b * ADDS + 1 + (0 if pair < 2 else max(pair - 2, 1)))
                down = ps_down[pair % SLOTS][:, :].rearrange("p (a q h) -> p a q h", a=2, q=TILES)
                by_gate = gates[:, :, 2 * pair:2 * pair + 2].rearrange("p q a -> p a q").unsqueeze(3).to_broadcast([PARTS, 2, TILES, H])
                nc.vector.tensor_tensor(scaled[:, pair % SLOTS, :, :].rearrange("p a (q h) -> p a q h", q=TILES),
                                        down, by_gate, ALU.mult).then_inc(scaled_made, 1)

            def add_base(b):
                dve.wait_ge(b2_ps, b + 1)
                nc.vector.tensor_tensor(tiles(y_base, b), small_h, z2[:, :, 0, :], ALU.add).then_inc(y_base_made, 1)

            def finish_ffn(b):
                dve.wait_ge(moe_added, b * ADDS + ADDS + 1)
                halves = [moe[:, a, :].rearrange("p (q h) -> p q h", q=TILES) for a in range(2)]
                nc.vector.tensor_tensor(moe_sum[:, :, :], halves[0], halves[1], ALU.add).then_inc(moe_read, 1)
                dve.wait_ge(moe_read, b + 2)
                dve.wait_ge(y_base_made, b + 1)
                e_link(nc.vector.tensor_tensor(y[:, :, :], moe_sum[:, :, :], tiles(y_base, b), ALU.add), b)
                normalise(2, b, y[:, :, :], e_link)

            def write_y(b):
                dve.wait_ge(rstd_made[2], b + 1)
                t = ln[2]
                dve.wait_ge(out_stored, 16 * b + 1)
                e_link(nc.vector.tensor_tensor(y_norm[:, :, :], t["cen"][:, :, :], over_h(t["rstd"][:, :]), ALU.mult), b)
                e_link(nc.vector.tensor_tensor(y_gam[:, :, :], y_norm[:, :, :],
                                               gamma_bc[:, :].unsqueeze(1).to_broadcast([PARTS, TILES, H]), ALU.mult), b)
                dve.wait_ge(h1_beta_made, b + 1)
                nc.vector.tensor_tensor(y_out[:, :, :], y_gam[:, :, :], tiles(h1_beta, b), ALU.add).then_inc(out_made, 1)

            def iteration(front, ffn):
                count.clear()
                if ffn is not None:
                    scale_pair(ffn, 0)
                    add_base(ffn)
                if front is not None:
                    mark_edges(front)
                    copy_windows(front, 1)
                    copy_windows(front, 3)
                if ffn is not None:
                    scale_pair(ffn, 1)
                if front is not None:
                    norm_h0(front)
                if ffn is not None:
                    scale_pair(ffn, 2)
                if front is not None:
                    make_z1(front)
                if ffn is not None:
                    scale_pair(ffn, 3)
                if front is not None:
                    split_z1(front)
                if ffn is not None:
                    scale_pair(ffn, 4)
                if front is not None:
                    scores(front)
                    make_probs(front)
                if ffn is not None:
                    scale_pair(ffn, 5)
                if front is not None:
                    finish_attention(front)
                if ffn is not None:
                    scale_pair(ffn, 6)
                if front is not None:
                    make_z2(front)
                if ffn is not None:
                    scale_pair(ffn, 7)
                if front is not None:
                    split_z2(front)
                if ffn is not None:
                    finish_ffn(ffn)
                if front is not None:
                    choose_experts(front)
                if ffn is not None:
                    write_y(ffn)
                assert front is None or count[front_chain] == FRONT_LINKS, count[front_chain]
                assert ffn is None or count[ffn_chain] == FFN_LINKS, count[ffn_chain]

            iteration(0, None)
            dve.wait_ge(w1_hi_made, 1)
            nc.vector.tensor_tensor(w1_lo[:, :], w1_raw[0:H, :], w1_hi[0:H, :].bitcast(f32), ALU.subtract).then_inc(w1_made, 1)
            dve.wait_ge(norm_in, 32)
            dve.sem_inc(scaled_made, SLOTS)
            dve.sem_inc(moe_read, 1)
            with dve.Fori(1, BATCHES) as b:
                iteration(b, b - 1)
            iteration(None, BATCHES - 1)


def kernel(x, L0_tok_emb, L0_tok_W, L0_tok_b, L0_attn_W, L0_attn_a, L0_ffn_gate_w, L0_ffn_gate_b, L0_ffn_w1,
           L0_ffn_b1, L0_ffn_w2, L0_ffn_b2, L0_ffn_gamma, L0_ffn_beta):
    import numpy as np
    import concourse.bacc as bacc
    from concourse import mybir
    from concourse.bass_utils import run_bass_kernel_spmd

    batches, seq = x.shape
    tiles = seq // PARTS
    taps_w = np.asarray(L0_tok_W)
    hidden = taps_w.shape[0]
    by_tile = np.asarray(x).reshape(batches, PARTS, tiles)
    arrays = {
        "ids": by_tile.transpose(1, 0, 2).reshape(PARTS, batches * tiles),
        "id_row": by_tile.transpose(0, 2, 1).reshape(1, batches * seq),
        "emb": np.asarray(L0_tok_emb),
        "conv_rows": taps_w.transpose(2, 1, 0).reshape(-1, hidden),
        "conv_taps": taps_w.transpose(1, 2, 0),
        "conv_b": np.asarray(L0_tok_b).reshape(1, -1),
        "att_w": np.asarray(L0_attn_W),
        "att_wt": np.asarray(L0_attn_W).T,
        "att_a": np.asarray(L0_attn_a).reshape(2, hidden).T,
        "gate_w": np.asarray(L0_ffn_gate_w),
        "gate_b": np.asarray(L0_ffn_gate_b).reshape(1, -1),
        "w1": np.asarray(L0_ffn_w1).transpose(1, 0, 2).reshape(hidden, -1),
        "b1": np.asarray(L0_ffn_b1).T,
        "w2": np.asarray(L0_ffn_w2).transpose(1, 0, 2),
        "b2": np.asarray(L0_ffn_b2),
        "gamma": np.asarray(L0_ffn_gamma).reshape(1, -1),
        "beta": np.asarray(L0_ffn_beta).reshape(1, -1),
    }
    arrays = {name: np.ascontiguousarray(a) for name, a in arrays.items()}
    nc = bacc.Bacc("TRN2", target_bir_lowering=False, num_devices=1)
    args = {name: nc.dram_tensor(f"in_{name}", a.shape, mybir.dt.from_np(a.dtype), kind="ExternalInput").ap()
            for name, a in arrays.items()}
    out = nc.dram_tensor("out", (batches, seq, hidden), mybir.dt.float32, kind="ExternalOutput").ap()
    tower(nc, out=out, **args)
    r = run_bass_kernel_spmd(nc, [{f"in_{name}": a for name, a in arrays.items()}], core_ids=[0])
    return r.results[0]["out"]
```

```python
import concourse.bass as bass
from concourse import mybir
from contextlib import ExitStack

PARTS = 128


def tower(nc, ids, id_row, emb, conv_rows, conv_taps, conv_b, att_w, att_wt, att_a,
          gate_w, gate_b, w1, b1, w2, b2, gamma, beta, out):
    f32, f32r, i32, u32 = mybir.dt.float32, mybir.dt.float32r, mybir.dt.int32, mybir.dt.uint32
    ALU, ACT, AX = mybir.AluOpType, mybir.ActivationFunctionType, mybir.AxisListType.X

    VOCAB, H = emb.shape
    TAPS = conv_taps.shape[1]
    HALF = TAPS // 2
    BATCHES, SEQ, _ = out.shape
    TILES = SEQ // PARTS
    E, F = b1.shape[1], b1.shape[0]
    PAIRS = E // 2
    ADDS = PAIRS - 1
    WIN = TAPS * H
    FULL = WIN // PARTS
    REST = WIN - FULL * PARTS
    EDGE = 4 * HALF
    BIAS_ROW = REST + EDGE
    LAST = BIAS_ROW + 1
    NH = H + 2
    GROW = 32
    ALPHA, EPS = 0.01, 1e-5
    UP_SLOTS = 2
    HIDDEN_PAIRS = 2
    BC_SLOTS = 2
    SUM_SLOTS = 4

    ctx = ExitStack()
    with ctx:
        def sb(name, shape, dt=f32):
            return ctx.enter_context(nc.sbuf_tensor(name, shape, dt))

        def sem(name):
            return ctx.enter_context(nc.semaphore(name))

        ident = sb("ident", [PARTS, PARTS])
        minus_half = sb("minus_half", [PARTS, TILES])
        expert_no = sb("expert_no", [PARTS, TILES, E])
        fold = sb("fold", [PARTS, H])
        spread_no = sb("spread_no", [2 * GROW, PAIRS, PARTS])
        spread = sb("spread", [2 * GROW, PAIRS, PARTS], f32r)
        id_cols = sb("id_cols", [PARTS, BATCHES * TILES], i32)
        window_at = sb("window_at", [PARTS, BATCHES * TILES], i32)
        window_now = sb("window_now", [PARTS, TILES], i32)
        id_bc = sb("id_bc", [REST + EDGE, BATCHES * SEQ], i32)
        edge_no = sb("edge_no", [REST + EDGE, 1])
        edge_high = sb("edge_high", [REST + EDGE, 1])
        edge_id = sb("edge_id", [REST + EDGE, 1])
        NV = TAPS + 2 * HALF
        edge_rows = sb("edge_rows", [2 * NV, H])
        edge_rows_t = sb("edge_rows_t", [H, 2 * NV])
        edge_diff = sb("edge_diff", [H, TAPS, EDGE])
        taps = sb("taps", [H, TAPS, H])
        conv_w = sb("conv_w", [PARTS, FULL, H])
        conv_w_last = sb("conv_w_last", [LAST, H])
        att_wt_dup = sb("att_wt_dup", [H, 2, H])
        a_cols = sb("a_cols", [H, 2])
        a_rep = sb("a_rep", [H, 2 + 2 * PARTS])
        wh_raw = sb("wh_raw", [PARTS, NH])
        wh_hi = sb("wh_hi", [PARTS, NH], f32r)
        wh_lo = sb("wh_lo", [H, NH], f32r)
        wf_hi = sb("wf_hi", [PARTS, 2, PARTS], f32r)
        wf_lo = sb("wf_lo", [H, 2, PARTS], f32r)
        gate_raw = sb("gate_raw", [PARTS, E])
        gate_hi = sb("gate_hi", [PARTS, E], f32r)
        gate_lo = sb("gate_lo", [H, E], f32r)
        gate_bias = sb("gate_bias", [PARTS, E])
        w1_raw = sb("w1_raw", [PARTS, E * F])
        w1_hi = sb("w1_hi", [PARTS, E * F], f32r)
        w1_lo = sb("w1_lo", [H, E * F], f32r)
        b1_cols = sb("b1_cols", [F, E])
        w2_sb = sb("w2_sb", [F, E, H])
        b2_cols = sb("b2_cols", [PARTS, PAIRS])
        gamma_bc = sb("gamma_bc", [PARTS, H])
        beta_bc = sb("beta_bc", [PARTS, H])

        win = sb("win", [PARTS, TILES, WIN])
        win_t = sb("win_t", [PARTS, TILES, FULL, PARTS])
        win_t_last = sb("win_t_last", [96, SEQ])
        conv_out = sb("conv_out", [PARTS, SEQ // 2])
        h0 = sb("h0", [PARTS, TILES, H])
        z1 = sb("z1", [PARTS, TILES, H])
        z1_t = sb("z1_t", [PARTS, SEQ], f32r)
        f2_max = sb("f2_max", [PARTS, 1])
        s_min = sb("s_min", [PARTS, SEQ])
        s_max = sb("s_max", [PARTS, SEQ])
        exp_a = sb("exp_a", [PARTS, SEQ])
        exp_b = sb("exp_b", [PARTS, SEQ])
        f2_diff = sb("f2_diff", [PARTS, TILES])
        exp_r = sb("exp_r", [PARTS, TILES])
        hv = sb("hv", [PARTS, TILES, H + 1])
        probs = sb("probs", [PARTS, TILES, SEQ])
        rden = sb("rden", [PARTS, TILES])
        att = sb("att", [PARTS, TILES, H])
        att_neg = sb("att_neg", [PARTS, TILES, H])
        att_exp = sb("att_exp", [PARTS, TILES, H])
        att_res = sb("att_res", [PARTS, TILES, H])
        h1 = sb("h1", [PARTS, TILES, H])
        z2 = sb("z2", [PARTS, TILES, H])
        z2_t = sb("z2_t", [PARTS, SEQ], f32r)
        logits = sb("logits", [PARTS, TILES, E])
        top = sb("top", [PARTS, TILES, 8])
        top_at = sb("top_at", [PARTS, TILES, 8], u32)
        top_no = sb("top_no", [PARTS, TILES, 2])
        gap = sb("gap", [PARTS, TILES])
        gap_exp = sb("gap_exp", [PARTS, TILES])
        gap_sum = sb("gap_sum", [PARTS, TILES])
        gate_1 = sb("gate_1", [PARTS, TILES])
        gate_2 = sb("gate_2", [PARTS, TILES])
        is_1 = sb("is_1", [PARTS, TILES, E])
        is_2 = sb("is_2", [PARTS, TILES, E])
        gates = sb("gates", [PARTS, TILES, E])
        gates_t = sb("gates_t", [2 * GROW, SEQ], f32r)
        ln = [dict(stats=sb(f"ln{n}_stats", [PARTS, TILES, 6]), moments=sb(f"ln{n}_moments", [PARTS, TILES, 2]),
                   var=sb(f"ln{n}_var", [PARTS, TILES]), rstd=sb(f"ln{n}_rstd", [PARTS, TILES]))
              for n in range(3)]

        hidden = sb("hidden", [F, 2 * HIDDEN_PAIRS, SEQ])
        gate_bc = sb("gate_bc", [PARTS, BC_SLOTS, SEQ])
        scaled = sb("scaled", [PARTS, SUM_SLOTS, SEQ])
        moe = sb("moe", [PARTS, SEQ])
        z2_kept = sb("z2_kept", [PARTS, BATCHES * TILES, H])
        h1_beta = sb("h1_beta", [PARTS, BATCHES * TILES, H])
        y = sb("y", [PARTS, TILES, H])
        y_norm = sb("y_norm", [PARTS, TILES, H])
        y_gam = sb("y_gam", [PARTS, TILES, H])
        y_out = sb("y_out", [PARTS, TILES, H])

        bank = [ctx.enter_context(nc.psum_tensor(f"bank{n}", [PARTS, 512], f32)) for n in range(8)]
        ps_a, ps_b, ps_small, ps_wide = bank[0], bank[1], bank[2], bank[7]
        ps_up = bank[3:5]
        ps_down, ps_bc = bank[5], bank[6]
        turn_bank = (ps_b, ps_a)
        turned_h = ps_small[:, 256:512].rearrange("p (t a h) -> p a t h", t=2, a=2)
        small_nh = ps_small[:, 0:TILES * NH].rearrange("p (q h) -> p q h", q=TILES)
        att_ps = ps_a[:, 0:TILES * (H + 1)].rearrange("p (q h) -> p q h", q=TILES)
        folded = ps_down[:, 0:TILES * H].rearrange("p (q h) -> p q h", q=TILES)

        ids_in, rows_in, edge_in, conv_in, att_in, gate_in, w1_in, ffn_in, norm_in = [
            sem(n) for n in ("ids_in", "rows_in", "edge_in", "conv_in", "att_in", "gate_in", "w1_in",
                             "ffn_in", "norm_in")]
        const_made, ident_made, windows_known, edge_known = [
            sem(n) for n in ("const_made", "ident_made", "windows_known", "edge_known")]
        window_copied = sem("window_copied")
        setup_chain = sem("setup_chain")
        edge_rows_ps, edge_rows_sb, edge_diff_sb, edge_ps, conv_w_made = [
            sem(n) for n in ("edge_rows_ps", "edge_rows_sb", "edge_diff_sb", "edge_ps", "conv_w_made")]
        a_rep_made, wa_ps, wa_hi_made, wa_made, gate_hi_made, gate_made, w1_hi_made, w1_made = [
            sem(n) for n in ("a_rep_made", "wa_ps", "wa_hi_made", "wa_made", "gate_hi_made", "gate_made",
                             "w1_hi_made", "w1_made")]
        gathered = [sem(f"gathered{q}") for q in range(TILES)]
        win_t_ps, win_t_act, win_t_dve, win_t_rest, edge_hot, conv_ps = [
            sem(n) for n in ("win_t_ps", "win_t_act", "win_t_dve", "win_t_rest", "edge_hot", "conv_ps")]
        h0_saved, z1_made, z1_t_ps, z1_hi_made, z1_t_made, f2_ps, f1_ps, h_ps = [
            sem(n) for n in ("h0_saved", "z1_made", "z1_t_ps", "z1_hi_made", "z1_t_made", "f2_ps", "f1_ps",
                             "h_ps")]
        s_min_made, s_max_made, f2_diff_made, exp_a_made, exp_b_made, exp_r_made, exp_v_made = [
            sem(n) for n in ("s_min_made", "s_max_made", "f2_diff_made", "exp_a_made", "exp_b_made",
                             "exp_r_made", "exp_v_made")]
        probs_made, hv_made, att_done, att_made, att_neg_made, att_exp_made, h1_made, h1_beta_made = [
            sem(n) for n in ("probs_made", "hv_made", "att_done", "att_made", "att_neg_made", "att_exp_made", "h1_made",
                             "h1_beta_made")]
        z2_made, z2_t_ps, z2_hi_made, z2_t_made, logits_ps, gap_made, gap_exp_made, gates_made = [
            sem(n) for n in ("z2_made", "z2_t_ps", "z2_hi_made", "z2_t_made", "logits_ps", "gap_made",
                             "gap_exp_made", "gates_made")]
        stats_made = [sem(f"stats_made{n}") for n in range(3)]
        var_made = [sem(f"var_made{n}") for n in range(3)]
        rstd_made = [sem(f"rstd_made{n}") for n in range(3)]
        gates_t_ps, gates_hi_made, gates_t_made, z2_kept_made, conv_out_made, turned_ps = [
            sem(n) for n in ("gates_t_ps", "gates_hi_made", "gates_t_made", "z2_kept_made", "conv_out_made", "turned_ps")]
        up_ps, hidden_made, down_ps, bc_ps, bc_made, scaled_made, moe_added, fold_ps, y_made, out_made, out_stored = [
            sem(n) for n in ("up_ps", "hidden_made", "down_ps", "bc_ps", "bc_made", "scaled_made", "moe_added",
                             "fold_ps", "y_made", "out_made", "out_stored")]
        logits_made, spread_made = sem("logits_made"), sem("spread_made")
        front_chain, norm_chain, ffn_chain = sem("front_chain"), sem("norm_chain"), sem("ffn_chain")

        block = ctx.enter_context(nc.Block())

        def tiles(t, b):
            return t[:, bass.ds(b * TILES, TILES), :]

        def over_h(t, n=H):
            return t.unsqueeze(2).to_broadcast([PARTS, TILES, n])

        @block.sync
        def _(sp):
            sp.dma_start(id_cols[:, :], ids).then_inc(ids_in, 16)
            sp.dma_start(id_bc[REST:REST + EDGE, :], id_row.to_broadcast([EDGE, BATCHES * SEQ])).then_inc(rows_in, 16)
            sp.dma_start(taps[:, :, :], conv_taps).then_inc(edge_in, 16)
            sp.dma_start(conv_w[:, :, :], conv_rows[0:FULL * PARTS, :].rearrange("(c p) o -> p c o", p=PARTS)).then_inc(conv_in, 16)
            sp.dma_start(conv_w_last[0:REST, :], conv_rows[FULL * PARTS:WIN, :]).then_inc(conv_in, 16)
            sp.dma_start(conv_w_last[BIAS_ROW:LAST, :], conv_b).then_inc(conv_in, 16)
            sp.dma_start(w1_raw[0:H, :], w1).then_inc(w1_in, 16)
            sp.dma_start(w1_raw[H:2 * H, :], w1).then_inc(w1_in, 16)
            sp.dma_start(w2_sb[:, :, :], w2).then_inc(ffn_in, 16)
            sp.dma_start(b1_cols[:, :], b1).then_inc(ffn_in, 16)
            sp.dma_start(b2_cols[:, :], b2).then_inc(ffn_in, 16)
            sp.dma_start(beta_bc[:, :], beta.to_broadcast([PARTS, H])).then_inc(norm_in, 16)
            sp.dma_start(gamma_bc[:, :], gamma.to_broadcast([PARTS, H])).then_inc(norm_in, 16)
            sp.sem_inc(out_stored, 1)
            with sp.Fori(0, BATCHES) as b:
                sp.wait_ge(out_made, b + 1)
                sp.dma_start(out[bass.ds(b, 1), :, :].rearrange("a (p q) h -> p (a q h)", q=TILES),
                             y_out[:, :, :].rearrange("p q h -> p (q h)")).then_inc(out_stored, 16)
            sp.wait_ge(out_stored, 16 * BATCHES + 1)

        @block.gpsimd
        def _(pool):
            pool.memset(ident[:, :], 0.0).then_inc(ident_made, 1)
            pool.memset(minus_half[:, :], -0.5).then_inc(const_made, 1)
            pool.wait_ge(ident_made, 1)
            pool.affine_select(out=ident[:, :], in_=ident[:, :], compare_op=ALU.not_equal, fill=1.0, base=0,
                               pattern=[[-1, PARTS]], channel_multiplier=1).then_inc(ident_made, 1)
            pool.wait_ge(ident_made, 2)
            pool.iota(spread_no[0:GROW, :, :], pattern=[[2, PAIRS], [1, 2], [0, H]], base=0, channel_multiplier=-1,
                      allow_small_or_imprecise_dtypes=True).then_inc(const_made, 1)
            pool.iota(spread_no[GROW:2 * GROW, :, :], pattern=[[2, PAIRS], [1, 2], [0, H]], base=0, channel_multiplier=-1,
                      allow_small_or_imprecise_dtypes=True).then_inc(const_made, 1)
            pool.iota(edge_no[REST:REST + EDGE, :], pattern=[[0, 1]], base=0, channel_multiplier=1,
                      allow_small_or_imprecise_dtypes=True).then_inc(const_made, 1)

            def gather(b, q):
                pool.indirect_dma_start(win[:, q, :], None, emb,
                                        bass.IndirectOffsetOnAxis(ap=window_at[:, b * TILES + q:b * TILES + q + 1], axis=0)
                                        ).then_inc(gathered[q], 16)

            def gather_next(b, tiles_now):
                for q in tiles_now:
                    pool.wait_ge(windows_known, 2)
                    pool.wait_ge(win_t_ps, b * TILES + q + 1)
                    pool.tensor_copy(window_now[:, q:q + 1], window_at[:, bass.ds((b + 1) * TILES + q, 1)]).then_inc(window_copied, 1)
                    pool.wait_ge(windows_known, 2)
                    pool.wait_ge(window_copied, b * TILES + q + 1)
                    pool.indirect_dma_start(win[:, q, :], None, emb,
                                            bass.IndirectOffsetOnAxis(ap=window_now[:, q:q + 1], axis=0)
                                            ).then_inc(gathered[q], 16)

            def inverse_deviation(n, b):
                pool.wait_ge(var_made[n], b + 1)
                pool.tensor_tensor(ln[n]["rstd"][:, :], ln[n]["var"][:, :], minus_half[:, :], ALU.pow).then_inc(rstd_made[n], 1)

            def add_pair(b, pair):
                pool.wait_ge(scaled_made, b * PAIRS + pair + 1 + BC_SLOTS)
                now = scaled[:, pair % SUM_SLOTS, :]
                if pair == 1:
                    pool.wait_ge(fold_ps, b + 1)
                    pool.tensor_tensor(moe[:, :], scaled[:, 0, :], now, ALU.add).then_inc(moe_added, 1)
                else:
                    pool.wait_ge(moe_added, b * ADDS + pair)
                    pool.tensor_tensor(moe[:, :], moe[:, :], now, ALU.add).then_inc(moe_added, 1)

            def add_beta(b):
                pool.wait_ge(h1_made, b + 1)
                pool.tensor_tensor(tiles(h1_beta, b), h1[:, :, :],
                                   beta_bc[:, :].unsqueeze(1).to_broadcast([PARTS, TILES, H]), ALU.add).then_inc(h1_beta_made, 1)

            def iteration(front, ffn, ahead, gather_more):
                if ffn is not None:
                    for pair in range(1, 4):
                        add_pair(ffn, pair)
                if front is not None:
                    inverse_deviation(1, front)
                    add_beta(front)
                if gather_more:
                    gather_next(ahead, range(0, TILES // 2))
                if ffn is not None:
                    add_pair(ffn, 4)
                if gather_more:
                    gather_next(ahead, range(TILES // 2, TILES))
                if ffn is not None:
                    add_pair(ffn, 5)
                if ahead is not None:
                    inverse_deviation(0, ahead)
                if ffn is not None:
                    add_pair(ffn, 6)
                    add_pair(ffn, 7)
                    inverse_deviation(2, ffn)

            pool.wait_ge(windows_known, 2)
            for q in range(TILES):
                gather(0, q)
            gather_next(0, range(TILES))
            pool.wait_ge(const_made, 4)
            inverse_deviation(0, 0)
            pool.wait_ge(norm_in, 32)
            pool.sem_inc(moe_added, 1)
            iteration(0, None, 1, True)
            with pool.Fori(1, BATCHES - 2) as b:
                iteration(b, b - 1, b + 1, True)
            iteration(BATCHES - 2, BATCHES - 3, BATCHES - 1, False)
            iteration(BATCHES - 1, BATCHES - 2, None, False)
            iteration(None, BATCHES - 1, None, False)

        @block.scalar
        def _(act):
            act.dma_start(edge_rows[0:2 * HALF, :], emb[0:1, :].to_broadcast([2 * HALF, H])).then_inc(edge_in, 16)
            act.dma_start(edge_rows[2 * HALF:NV, :], emb[0:TAPS, :]).then_inc(edge_in, 16)
            act.dma_start(edge_rows[NV:NV + TAPS, :], emb[VOCAB - TAPS:VOCAB, :]).then_inc(edge_in, 16)
            act.dma_start(edge_rows[NV + TAPS:2 * NV, :], emb[VOCAB - 1:VOCAB, :].to_broadcast([2 * HALF, H])).then_inc(edge_in, 16)
            act.dma_start(a_cols[:, :], att_a).then_inc(att_in, 16)
            act.dma_start(att_wt_dup[:, 0, :], att_wt).then_inc(att_in, 16)
            act.dma_start(att_wt_dup[:, 1, :], att_wt).then_inc(att_in, 16)
            act.dma_start(wh_raw[0:H, 0:H], att_w).then_inc(att_in, 16)
            act.dma_start(wh_raw[H:2 * H, 0:H], att_w).then_inc(att_in, 16)
            act.dma_start(gate_raw[0:H, :], gate_w).then_inc(gate_in, 16)
            act.dma_start(gate_raw[H:2 * H, :], gate_w).then_inc(gate_in, 16)
            act.dma_start(gate_bias[:, :], gate_b.to_broadcast([PARTS, E])).then_inc(gate_in, 16)

            act.wait_ge(edge_rows_ps, 1)
            act.activation(edge_rows_t[:, :], ps_up[0][0:H, 0:2 * NV], ACT.Copy).then_inc(edge_rows_sb, 1)
            act.wait_ge(wa_ps, 1)
            act.activation(wh_raw[:, H:NH], ps_down[:, 0:2], ACT.Copy).then_inc(wa_hi_made, 1)
            act.activation(wf_hi[:, :, :].rearrange("p a b -> p (a b)"), ps_down[:, 2:2 + 2 * PARTS], ACT.Copy).then_inc(wa_hi_made, 1)
            act.wait_ge(att_in, 16 * 5)
            act.wait_ge(wa_hi_made, 2)
            act.activation(wh_hi[:, :], wh_raw[:, :], ACT.Copy).then_inc(wa_hi_made, 1)
            act.wait_ge(gate_in, 16 * 3)
            act.activation(gate_hi[:, :], gate_raw[:, :], ACT.Copy).then_inc(gate_hi_made, 1)

            def copy_windows(b, q):
                act.wait_ge(win_t_ps, b * TILES + q + 1)
                act.activation(win_t[:, q, :, :].rearrange("p c t -> p (c t)"), turn_bank[q % 2][:, :], ACT.Copy).then_inc(win_t_act, 1)

            def copy_last_rows(b):
                act.wait_ge(win_t_ps, b * TILES + TILES)
                act.activation(win_t_last[0:REST, :], ps_wide[0:REST, :], ACT.Copy).then_inc(win_t_rest, 1)

            def copy_convolution(b):
                act.wait_ge(conv_ps, b + 1)
                act.activation(conv_out[:, :], ps_small[:, 0:SEQ // 2], ACT.Copy).then_inc(conv_out_made, 1)

            def save_h0(b):
                act.wait_ge(turned_ps, b + 1)
                act.activation(h0[:, :, :].rearrange("p (a t) h -> p a t h", a=2), turned_h, ACT.Copy).then_inc(h0_saved, 1)

            def round_z1(b):
                act.wait_ge(z1_t_ps, b + 1)
                act.activation(z1_t[0:H, :], ps_a[0:H, :], ACT.Copy).then_inc(z1_hi_made, 1)

            def exps(b):
                act.wait_ge(s_min_made, b + 1)
                act.activation(exp_a[:, :], s_min[:, :], ACT.Exp, scale=1.0 - ALPHA).then_inc(exp_a_made, 1)
                act.wait_ge(f2_diff_made, b + 1)
                act.activation(exp_r[:, :], f2_diff[:, :], ACT.Exp, scale=1.0 - ALPHA).then_inc(exp_r_made, 1)
                act.activation(hv[:, :, H:H + 1], f2_diff[:, :].unsqueeze(2), ACT.Exp, scale=ALPHA).then_inc(exp_v_made, 1)
                act.wait_ge(s_max_made, b + 1)
                act.activation(exp_b[:, :], s_max[:, :], ACT.Exp, scale=-(1.0 - ALPHA)).then_inc(exp_b_made, 1)

            def exp_negative_part(b):
                act.wait_ge(att_neg_made, b + 1)
                act.activation(att_exp[:, :, :], att_neg[:, :, :], ACT.Exp).then_inc(att_exp_made, 1)

            def round_z2(b):
                act.wait_ge(z2_t_ps, b + 1)
                act.activation(z2_t[0:H, :], ps_b[0:H, :], ACT.Copy).then_inc(z2_hi_made, 1)
                act.activation(tiles(z2_kept, b), z2[:, :, :], ACT.Copy).then_inc(z2_kept_made, 1)

            def exp_gap(b):
                act.wait_ge(gap_made, b + 1)
                act.activation(gap_exp[:, :], gap[:, :], ACT.Exp).then_inc(gap_exp_made, 1)

            def round_gates(b):
                act.wait_ge(gates_t_ps, b + 1)
                act.activation(gates_t[0:E, :], ps_wide[0:E, :], ACT.Copy).then_inc(gates_hi_made, 1)

            def hide(b, pair):
                for e in (2 * pair, 2 * pair + 1):
                    act.wait_ge(up_ps, b * E + e + 1)
                    act.wait_ge(down_ps, b * PAIRS + pair + 1)
                    act.activation(hidden[:, e % (2 * HIDDEN_PAIRS), :], ps_up[e % UP_SLOTS][:, :], ACT.Relu,
                                   bias=b1_cols[:, e:e + 1]).then_inc(hidden_made, 1)

            def copy_gates(b, pair):
                act.wait_ge(bc_ps, b * PAIRS + pair + 1)
                act.wait_ge(scaled_made, b * PAIRS + pair + 1)
                act.activation(gate_bc[:, pair % BC_SLOTS, :], ps_bc[:, :], ACT.Copy).then_inc(bc_made, 1)

            def step(b, pair):
                if b is None:
                    return
                if pair + 1 < PAIRS:
                    hide(b, pair + 1)
                copy_gates(b, pair)

            def turn_windows(b):
                copy_windows(b, 0)
                copy_windows(b, 2)
                copy_last_rows(b)

            def iteration(front, ffn, ahead):
                if ffn is not None:
                    hide(ffn, 0)
                    round_gates(ffn)
                step(ffn, 0)
                if front is not None:
                    round_z1(front)
                step(ffn, 1)
                if front is not None:
                    exps(front)
                step(ffn, 2)
                step(ffn, 3)
                if front is not None:
                    exp_negative_part(front)
                if ahead is not None:
                    turn_windows(ahead)
                step(ffn, 4)
                if ahead is not None:
                    copy_convolution(ahead)
                step(ffn, 5)
                if ahead is not None:
                    save_h0(ahead)
                step(ffn, 6)
                if front is not None:
                    round_z2(front)
                step(ffn, 7)
                if front is not None:
                    exp_gap(front)

            turn_windows(0)
            copy_convolution(0)
            save_h0(0)
            act.wait_ge(w1_in, 32)
            act.activation(w1_hi[:, :], w1_raw[:, :], ACT.Copy).then_inc(w1_hi_made, 1)
            act.sem_inc(hidden_made, UP_SLOTS)
            act.sem_inc(bc_made, 1)
            iteration(0, None, 1)
            act.wait_ge(ffn_in, 48)
            with act.Fori(1, BATCHES - 1) as b:
                iteration(b, b - 1, b + 1)
            iteration(BATCHES - 1, BATCHES - 2, None)
            iteration(None, BATCHES - 1, None)

        @block.tensor
        def _(pe):
            def split_matmul(dst, lhs, lhs_lo, rhs, rhs_lo):
                nc.tensor.matmul(dst, lhs, rhs, start=True, stop=False)
                return nc.tensor.matmul(dst, lhs_lo, rhs_lo, start=False, stop=True)

            pe.sem_inc(down_ps, HIDDEN_PAIRS)
            pe.sem_inc(fold_ps, 1)
            pe.wait_ge(ident_made, 2)
            pe.wait_ge(edge_in, 16 * 5)
            nc.tensor.transpose(ps_up[0][0:H, 0:2 * NV], edge_rows[:, :], ident[0:2 * NV, 0:2 * NV]).then_inc(edge_rows_ps, 1)
            pe.wait_ge(a_rep_made, 3)
            nc.tensor.matmul(ps_down[:, 0:2 + 2 * PARTS], att_wt_dup[:, :, :].rearrange("f a h -> f (a h)"), a_rep[:, :],
                             start=True, stop=True).then_inc(wa_ps, 1)
            pe.wait_ge(edge_diff_sb, 1)
            for k in range(TAPS):
                last = nc.tensor.matmul(ps_up[1][REST:REST + EDGE, 0:H], edge_diff[:, k, :], taps[:, k, :],
                                        start=(k == 0), stop=(k == TAPS - 1))
            last.then_inc(edge_ps, 1)

            def turn_windows(b):
                for q in range(TILES):
                    pe.wait_ge(gathered[q], 16 * (b + 1))
                    if q == 0:
                        pe.wait_ge(s_max_made, b)
                    elif q == 1:
                        pe.wait_ge(att_made, b)
                    elif q == 2:
                        pe.wait_ge(win_t_act, 2 * b + 1)
                    else:
                        pe.wait_ge(win_t_dve, 2 * b + 1)
                    for c in range(FULL):
                        nc.tensor.transpose(turn_bank[q % 2][:, c * PARTS:(c + 1) * PARTS],
                                            win[:, q, c * PARTS:(c + 1) * PARTS], ident[:, :])
                    nc.tensor.transpose(ps_wide[0:REST, q * PARTS:(q + 1) * PARTS],
                                        win[:, q, FULL * PARTS:WIN], ident[:, :]).then_inc(win_t_ps, 1)

            def convolve(b):
                pe.wait_ge(win_t_act, 2 * b + 2)
                pe.wait_ge(win_t_dve, 2 * b + 2)
                pe.wait_ge(win_t_rest, b + 1)
                pe.wait_ge(edge_hot, b + 1)
                weights = [conv_w[:, c, :] for c in range(FULL)] + [conv_w_last[:, :]]
                for c, w in enumerate(weights):
                    for a in range(2):
                        if c < FULL:
                            windows = win_t[:, 2 * a:2 * a + 2, c, :]
                        else:
                            windows = win_t_last[0:LAST, a * SEQ // 2:(a + 1) * SEQ // 2]
                        last = nc.tensor.matmul(ps_small[a * H:(a + 1) * H, 0:SEQ // 2], w, windows,
                                                start=(c == 0), stop=(c == FULL))
                last.then_inc(conv_ps, 1)

            def turn_convolution(b):
                pe.wait_ge(conv_out_made, b + 1)
                for t in range(2):
                    last = nc.tensor.transpose(ps_small[:, SEQ // 2 + t * PARTS:SEQ // 2 + (t + 1) * PARTS],
                                               conv_out[:, t * PARTS:(t + 1) * PARTS], ident[:, :])
                last.then_inc(turned_ps, 1)

            def turn_z1(b):
                pe.wait_ge(ident_made, 2)
                pe.wait_ge(z1_made, b + 1)
                for q in range(TILES):
                    last = nc.tensor.transpose(ps_a[0:H, q * PARTS:(q + 1) * PARTS], z1[:, q, :], ident[:, :])
                last.then_inc(z1_t_ps, 1)

            def project(b):
                pe.wait_ge(z1_t_made, b + 1)
                split_matmul(ps_wide[:, :], wf_hi[:, 1, :], wf_lo[:, 1, :], z1_t[:, :], z1_t[0:H, :]).then_inc(f2_ps, 1)
                split_matmul(ps_b[:, :], wf_hi[:, 0, :], wf_lo[:, 0, :], z1_t[:, :], z1_t[0:H, :]).then_inc(f1_ps, 1)
                pe.wait_ge(h0_saved, b + 1)
                for q in range(TILES):
                    cols = slice(q * PARTS, (q + 1) * PARTS)
                    last = split_matmul(small_nh[:, q, :], z1_t[:, cols], z1_t[0:H, cols], wh_hi[:, :], wh_lo[:, :])
                last.then_inc(h_ps, 1)

            def attend(b):
                pe.wait_ge(hv_made, b + 1)
                for j in range(TILES):
                    pe.wait_ge(probs_made, b * TILES + j + 1)
                    for i in range(TILES):
                        last = nc.tensor.matmul(att_ps[:, i, :], probs[:, j, i * PARTS:(i + 1) * PARTS], hv[:, j, :],
                                                start=(i == 0 and j == 0), stop=(i == TILES - 1 and j == TILES - 1),
                                                skip_group_check=True)
                last.then_inc(att_done, 1)

            def turn_z2(b):
                pe.wait_ge(ident_made, 2)
                pe.wait_ge(z2_made, b + 1)
                for q in range(TILES):
                    last = nc.tensor.transpose(ps_b[0:H, q * PARTS:(q + 1) * PARTS], z2[:, q, :], ident[:, :])
                last.then_inc(z2_t_ps, 1)

            def gate(b):
                pe.wait_ge(z2_t_made, b + 1)
                for q in range(TILES):
                    cols = slice(q * PARTS, (q + 1) * PARTS)
                    last = split_matmul(ps_wide[:, q * E:(q + 1) * E], z2_t[:, cols], z2_t[0:H, cols], gate_hi[:, :], gate_lo[:, :])
                last.then_inc(logits_ps, 1)

            def turn_gates(b):
                pe.wait_ge(gates_made, b + 1)
                for q in range(TILES):
                    last = nc.tensor.transpose(ps_wide[0:E, q * PARTS:(q + 1) * PARTS], gates[:, q, :], ident[:, :])
                last.then_inc(gates_t_ps, 1)

            def up(b, pair):
                for e in (2 * pair, 2 * pair + 1):
                    pe.wait_ge(hidden_made, b * E + e + 1)
                    split_matmul(ps_up[e % UP_SLOTS][:, :], w1_hi[:, e * F:(e + 1) * F], w1_lo[:, e * F:(e + 1) * F],
                                 z2_t[:, :], z2_t[0:H, :]).then_inc(up_ps, 1)

            def broadcast_gates(b, pair):
                if pair == 0:
                    pe.wait_ge(gates_t_made, b + 1)
                pe.wait_ge(bc_made, b * PAIRS + pair + 1)
                nc.tensor.matmul(ps_bc[:, :], spread[:, pair, :], gates_t[:, :], start=True, stop=True).then_inc(bc_ps, 1)

            def down(b, pair):
                if pair == 0:
                    pe.wait_ge(y_made, b + 1)
                else:
                    pe.wait_ge(scaled_made, b * PAIRS + pair + BC_SLOTS)
                pe.wait_ge(hidden_made, b * E + 2 * pair + 2 + UP_SLOTS)
                for a in range(2):
                    e = 2 * pair + a
                    last = nc.tensor.matmul(ps_down[a * H:(a + 1) * H, :], w2_sb[:, e, :], hidden[:, e % (2 * HIDDEN_PAIRS), :],
                                            start=True, stop=True)
                last.then_inc(down_ps, 1)

            def step(b, pair):
                if b is None:
                    return
                if pair + 1 < PAIRS:
                    up(b, pair + 1)
                broadcast_gates(b, pair)
                down(b, pair)

            def fold_experts(b):
                pe.wait_ge(moe_added, b * ADDS + ADDS + 1)
                for q in range(TILES):
                    last = nc.tensor.matmul(folded[:, q, :], moe[:, q * PARTS:(q + 1) * PARTS], fold[:, :], start=True, stop=True)
                last.then_inc(fold_ps, 1)

            def iteration(front, ffn, ahead):
                if ffn is not None:
                    up(ffn, 0)
                    turn_gates(ffn)
                step(ffn, 0)
                if front is not None:
                    turn_z1(front)
                step(ffn, 1)
                if front is not None:
                    project(front)
                step(ffn, 2)
                step(ffn, 3)
                if front is not None:
                    attend(front)
                if ahead is not None:
                    turn_windows(ahead)
                step(ffn, 4)
                if ahead is not None:
                    convolve(ahead)
                step(ffn, 5)
                if ahead is not None:
                    turn_convolution(ahead)
                step(ffn, 6)
                if front is not None:
                    turn_z2(front)
                step(ffn, 7)
                if front is not None:
                    gate(front)
                if ffn is not None:
                    fold_experts(ffn)

            turn_windows(0)
            pe.wait_ge(conv_in, 48)
            pe.wait_ge(conv_w_made, 1)
            convolve(0)
            turn_convolution(0)
            pe.wait_ge(wa_hi_made, 3)
            pe.wait_ge(wa_made, 2)
            pe.wait_ge(gate_hi_made, 1)
            pe.wait_ge(gate_made, 1)
            iteration(0, None, 1)
            pe.wait_ge(w1_hi_made, 1)
            pe.wait_ge(w1_made, 1)
            pe.wait_ge(ffn_in, 48)
            pe.wait_ge(spread_made, 2)
            with pe.Fori(2, BATCHES) as b:
                iteration(b - 1, b - 2, b)
            iteration(BATCHES - 1, BATCHES - 2, None)
            iteration(None, BATCHES - 1, None)

        @block.vector
        def _(dve):
            done = [0]

            def linked(ins):
                done[0] += 1
                ins.then_inc(setup_chain, 1)
                dve.wait_ge(setup_chain, done[0])

            dve.wait_ge(ids_in, 16)
            linked(nc.vector.tensor_scalar(window_at[:, :], id_cols[:, :], float(HALF), 0.0, ALU.subtract, ALU.max))
            nc.vector.tensor_scalar(window_at[:, :], window_at[:, :], float(VOCAB - TAPS), None, ALU.min).then_inc(windows_known, 2)
            nc.vector.memset(win_t_last[REST:96, :], 1.0).then_inc(setup_chain, 1)
            done[0] += 1
            dve.wait_ge(att_in, 16 * 5)
            nc.vector.tensor_copy(a_rep[:, 0:2], a_cols[:, 1:2].to_broadcast([H, 2])).then_inc(a_rep_made, 1)
            nc.vector.tensor_copy(a_rep[:, 2:2 + PARTS], a_cols[:, 0:1].to_broadcast([H, PARTS])).then_inc(a_rep_made, 1)
            nc.vector.tensor_copy(a_rep[:, 2 + PARTS:], a_cols[:, 1:2].to_broadcast([H, PARTS])).then_inc(a_rep_made, 1)
            dve.wait_ge(const_made, 4)
            edge = slice(REST, REST + EDGE)
            linked(nc.vector.tensor_scalar(edge_high[edge, :], edge_no[edge, :], 2.0 * HALF - 0.5, float(VOCAB - 2 * HALF),
                                           ALU.is_gt, ALU.mult))
            linked(nc.vector.scalar_tensor_tensor(edge_id[edge, :], edge_no[edge, :], float(-HALF), edge_high[edge, :], ALU.add, ALU.add))
            dve.wait_ge(rows_in, 16)
            linked(nc.vector.tensor_scalar(id_bc[edge, :], id_bc[edge, :], float(-HALF), float(VOCAB + HALF - 1), ALU.max, ALU.min))
            dve.wait_ge(edge_rows_sb, 1)
            for k in range(TAPS):
                for end, first, base in ((0, k, 2 * HALF + k), (1, NV + 1 + k, NV + k)):
                    last = nc.vector.tensor_scalar(edge_diff[:, k, end * 2 * HALF:(end + 1) * 2 * HALF],
                                                   edge_rows_t[:, first:first + 2 * HALF], edge_rows_t[:, base:base + 1],
                                                   None, ALU.subtract)
            last.then_inc(edge_diff_sb, 1)
            dve.wait_ge(edge_ps, 1)
            nc.vector.tensor_copy(conv_w_last[edge, :], ps_up[1][edge, 0:H]).then_inc(conv_w_made, 1)
            dve.wait_ge(wa_hi_made, 3)
            nc.vector.tensor_tensor(wh_lo[:, :], wh_raw[0:H, :], wh_hi[0:H, :].bitcast(f32), ALU.subtract).then_inc(wa_made, 1)
            nc.vector.tensor_tensor(wf_lo[:, :, :].rearrange("p a b -> p (a b)"), ps_down[0:H, 2:2 + 2 * PARTS],
                                    wf_hi[0:H, :, :].rearrange("p a b -> p (a b)").bitcast(f32), ALU.subtract).then_inc(wa_made, 1)
            dve.wait_ge(gate_hi_made, 1)
            nc.vector.tensor_tensor(gate_lo[:, :], gate_raw[0:H, :], gate_hi[0:H, :].bitcast(f32), ALU.subtract).then_inc(gate_made, 1)
            for e in range(E):
                last = nc.vector.memset(expert_no[:, :, e:e + 1], float(e))
            linked(last)
            nc.vector.memset(gates_t[:, :].bitcast(f32), 0.0)
            nc.vector.tensor_scalar(spread[:, :, :], spread_no[:, :, :], 0.0, None, ALU.is_equal).then_inc(spread_made, 1)
            nc.vector.tensor_copy(fold[0:H, :], ident[0:H, 0:H])
            nc.vector.tensor_copy(fold[H:2 * H, :], ident[H:2 * H, H:2 * H]).then_inc(spread_made, 1)

            FRONT_LINKS, NORM_LINKS, FFN_LINKS = 14, 1, 3
            count = {}

            def link(ins, b, chain, per):
                count[chain] = count.get(chain, 0) + 1
                ins.then_inc(chain, 1)
                dve.wait_ge(chain, b * per + count[chain])

            def f_link(ins, b):
                link(ins, b, front_chain, FRONT_LINKS)

            def n_link(ins, b):
                link(ins, b, norm_chain, NORM_LINKS)

            def e_link(ins, b):
                link(ins, b, ffn_chain, FFN_LINKS)

            def normalise(n, b, src, linker):
                t = ln[n]
                for q in range(TILES):
                    last = nc.vector.bn_stats(t["stats"][:, q, :], src[:, q, :])
                last.then_inc(stats_made[n], 1)
                dve.wait_ge(windows_known, 2)
                dve.wait_ge(stats_made[n], b + 1)
                for q in range(TILES):
                    last = nc.vector.bn_aggr(t["moments"][:, q, :], t["stats"][:, q, :])
                linker(last, b)
                nc.vector.tensor_scalar(t["var"][:, :].unsqueeze(2), t["moments"][:, :, 1:2], EPS, None, ALU.add).then_inc(var_made[n], 1)

            def scale(n, b, dst, src):
                dve.wait_ge(rstd_made[n], b + 1)
                for q in range(TILES):
                    last = nc.vector.tensor_scalar(dst[:, q, :], src[:, q, :], ln[n]["moments"][:, q, 0:1],
                                                   ln[n]["rstd"][:, q:q + 1], ALU.subtract, ALU.mult)
                return last

            def copy_windows(b, q):
                dve.wait_ge(win_t_ps, b * TILES + q + 1)
                nc.vector.tensor_copy(win_t[:, q, :, :].rearrange("p c t -> p (c t)"), turn_bank[q % 2][:, :]).then_inc(win_t_dve, 1)

            def mark_edges(b):
                dve.wait_ge(conv_ps, b)
                nc.vector.tensor_scalar(win_t_last[edge, :], id_bc[edge, bass.ds(b * SEQ, SEQ)], edge_id[edge, :], None,
                                        ALU.is_equal).then_inc(edge_hot, 1)

            def norm_h0(b):
                dve.wait_ge(h0_saved, b + 1)
                normalise(0, b, h0, n_link)

            def make_z1(b):
                scale(0, b, z1, h0).then_inc(z1_made, 1)

            def split_z1(b):
                dve.wait_ge(z1_hi_made, b + 1)
                nc.vector.tensor_tensor(z1_t[H:2 * H, :], ps_a[0:H, :], z1_t[0:H, :].bitcast(f32), ALU.subtract).then_inc(z1_t_made, 1)

            def scores(b):
                dve.wait_ge(f2_ps, b + 1)
                f_link(nc.vector.tensor_reduce(f2_max[:, :], ps_wide[:, :], axis=AX, op=ALU.max), b)
                dve.wait_ge(f1_ps, b + 1)
                nc.vector.tensor_scalar(s_min[:, :], ps_b[:, :], f2_max[:, :], 0.0, ALU.add, ALU.min).then_inc(s_min_made, 1)
                dve.wait_ge(h_ps, b + 1)
                nc.vector.tensor_scalar(f2_diff[:, :].unsqueeze(2), small_nh[:, :, H:H + 1], f2_max[:, :], None, ALU.subtract).then_inc(f2_diff_made, 1)
                nc.vector.tensor_scalar(s_max[:, :], ps_b[:, :], f2_max[:, :], 0.0, ALU.add, ALU.max).then_inc(s_max_made, 1)

            def make_probs(b):
                dve.wait_ge(exp_v_made, b + 1)
                nc.vector.tensor_tensor(hv[:, :, 0:H], small_nh[:, :, 0:H], hv[:, :, H:H + 1].to_broadcast([PARTS, TILES, H]),
                                        ALU.mult).then_inc(hv_made, 1)
                dve.wait_ge(exp_a_made, b + 1)
                dve.wait_ge(exp_r_made, b + 1)
                dve.wait_ge(exp_b_made, b + 1)
                for j in range(TILES):
                    nc.vector.scalar_tensor_tensor(probs[:, j, :], exp_a[:, :], exp_r[:, j:j + 1], exp_b[:, :],
                                                   ALU.mult, ALU.max).then_inc(probs_made, 1)

            def finish_attention(b):
                dve.wait_ge(att_done, b + 1)
                f_link(nc.vector.reciprocal(rden[:, :].unsqueeze(2), att_ps[:, :, H:H + 1]), b)
                nc.vector.tensor_tensor(att[:, :, :], att_ps[:, :, 0:H], over_h(rden[:, :]), ALU.mult).then_inc(att_made, 1)
                dve.wait_ge(att_made, b + 1)
                nc.vector.tensor_scalar(att_neg[:, :, :], att[:, :, :], 0.0, None, ALU.min).then_inc(att_neg_made, 1)
                dve.wait_ge(h0_saved, b + 1)
                f_link(nc.vector.scalar_tensor_tensor(att_res[:, :, :], att[:, :, :], 0.0, h0[:, :, :], ALU.max, ALU.add), b)
                dve.wait_ge(att_exp_made, b + 1)
                dve.wait_ge(h1_beta_made, b)
                nc.vector.scalar_tensor_tensor(h1[:, :, :], att_exp[:, :, :], -1.0, att_res[:, :, :], ALU.add, ALU.add).then_inc(h1_made, 1)
                dve.wait_ge(h1_made, b + 1)
                normalise(1, b, h1, f_link)

            def make_z2(b):
                scale(1, b, z2, h1).then_inc(z2_made, 1)

            def split_z2(b):
                dve.wait_ge(z2_hi_made, b + 1)
                nc.vector.tensor_tensor(z2_t[H:2 * H, :], ps_b[0:H, :], z2_t[0:H, :].bitcast(f32), ALU.subtract).then_inc(z2_t_made, 1)

            def choose_experts(b):
                dve.wait_ge(logits_ps, b + 1)
                nc.vector.tensor_tensor(logits[:, :, :], ps_wide[:, 0:TILES * E].rearrange("p (q e) -> p q e", q=TILES),
                                        gate_bias[:, :].unsqueeze(1).to_broadcast([PARTS, TILES, E]), ALU.add).then_inc(logits_made, 1)
                dve.wait_ge(windows_known, 2)
                dve.wait_ge(logits_made, b + 1)
                for q in range(TILES):
                    last = nc.vector.max(top[:, q, :], logits[:, q, :])
                f_link(last, b)
                nc.vector.tensor_tensor(gap[:, :].unsqueeze(2), top[:, :, 1:2], top[:, :, 0:1], ALU.subtract).then_inc(gap_made, 1)
                for q in range(TILES):
                    last = nc.vector.max_index(top_at[:, q, :], top[:, q, :], logits[:, q, :])
                f_link(last, b)
                f_link(nc.vector.tensor_copy(top_no[:, :, :], top_at[:, :, 0:2]), b)
                f_link(nc.vector.tensor_tensor(is_1[:, :, :], expert_no[:, :, :], top_no[:, :, 0:1].to_broadcast([PARTS, TILES, E]), ALU.is_equal), b)
                f_link(nc.vector.tensor_tensor(is_2[:, :, :], expert_no[:, :, :], top_no[:, :, 1:2].to_broadcast([PARTS, TILES, E]), ALU.is_equal), b)
                dve.wait_ge(gap_exp_made, b + 1)
                f_link(nc.vector.tensor_scalar(gap_sum[:, :], gap_exp[:, :], 1.0, None, ALU.add), b)
                f_link(nc.vector.reciprocal(gate_1[:, :], gap_sum[:, :]), b)
                f_link(nc.vector.tensor_tensor(gate_2[:, :], gap_exp[:, :], gate_1[:, :], ALU.mult), b)
                f_link(nc.vector.tensor_tensor(is_1[:, :, :], is_1[:, :, :], over_h(gate_1[:, :], E), ALU.mult), b)
                f_link(nc.vector.tensor_tensor(is_2[:, :, :], is_2[:, :, :], over_h(gate_2[:, :], E), ALU.mult), b)
                nc.vector.tensor_tensor(gates[:, :, :], is_1[:, :, :], is_2[:, :, :], ALU.add).then_inc(gates_made, 1)

            def split_gates(b):
                dve.wait_ge(gates_hi_made, b + 1)
                nc.vector.tensor_tensor(gates_t[GROW:GROW + E, :], ps_wide[0:E, :], gates_t[0:E, :].bitcast(f32), ALU.subtract).then_inc(gates_t_made, 1)

            def scale_pair(b, pair):
                if b is None:
                    return
                dve.wait_ge(down_ps, b * PAIRS + pair + 1 + HIDDEN_PAIRS)
                dve.wait_ge(bc_made, b * PAIRS + pair + 2)
                dve.wait_ge(moe_added, b * ADDS + 1 + (0 if pair < SUM_SLOTS else max(pair - SUM_SLOTS, 1)))
                nc.vector.scalar_tensor_tensor(scaled[:, pair % SUM_SLOTS, :], ps_down[:, :], b2_cols[:, pair:pair + 1],
                                               gate_bc[:, pair % BC_SLOTS, :], ALU.add, ALU.mult).then_inc(scaled_made, 1)

            def finish_ffn(b):
                dve.wait_ge(fold_ps, b + 2)
                dve.wait_ge(z2_kept_made, b + 1)
                nc.vector.tensor_tensor(y[:, :, :], folded, tiles(z2_kept, b), ALU.add).then_inc(y_made, 1)
                dve.wait_ge(y_made, b + 2)
                normalise(2, b, y, e_link)

            def write_y(b):
                dve.wait_ge(out_stored, 16 * b + 1)
                e_link(scale(2, b, y_norm, y), b)
                e_link(nc.vector.tensor_tensor(y_gam[:, :, :], y_norm[:, :, :],
                                               gamma_bc[:, :].unsqueeze(1).to_broadcast([PARTS, TILES, H]), ALU.mult), b)
                dve.wait_ge(h1_beta_made, b + 1)
                nc.vector.tensor_tensor(y_out[:, :, :], y_gam[:, :, :], tiles(h1_beta, b), ALU.add).then_inc(out_made, 1)

            def turn_windows(b):
                mark_edges(b)
                copy_windows(b, 1)
                copy_windows(b, 3)

            def iteration(front, ffn, ahead):
                if ffn is not None:
                    split_gates(ffn)
                scale_pair(ffn, 0)
                if front is not None:
                    split_z1(front)
                scale_pair(ffn, 1)
                if front is not None:
                    scores(front)
                scale_pair(ffn, 2)
                if front is not None:
                    make_probs(front)
                scale_pair(ffn, 3)
                if front is not None:
                    finish_attention(front)
                if ahead is not None:
                    turn_windows(ahead)
                if front is not None:
                    make_z2(front)
                scale_pair(ffn, 4)
                scale_pair(ffn, 5)
                if ahead is not None:
                    norm_h0(ahead)
                scale_pair(ffn, 6)
                if front is not None:
                    split_z2(front)
                scale_pair(ffn, 7)
                if front is not None:
                    choose_experts(front)
                if ffn is not None:
                    finish_ffn(ffn)
                if ahead is not None:
                    make_z1(ahead)
                if ffn is not None:
                    write_y(ffn)
                for chain, links, here in ((front_chain, FRONT_LINKS, front), (norm_chain, NORM_LINKS, ahead),
                                           (ffn_chain, FFN_LINKS, ffn)):
                    assert here is None or count.pop(chain) == links, (links, chain)
                count.clear()

            turn_windows(0)
            norm_h0(0)
            make_z1(0)
            count.clear()
            dve.sem_inc(scaled_made, BC_SLOTS)
            dve.sem_inc(y_made, 1)
            dve.wait_ge(w1_hi_made, 1)
            nc.vector.tensor_tensor(w1_lo[:, :], w1_raw[0:H, :], w1_hi[0:H, :].bitcast(f32), ALU.subtract).then_inc(w1_made, 1)
            iteration(0, None, 1)
            dve.wait_ge(norm_in, 32)
            with dve.Fori(1, BATCHES - 1) as b:
                iteration(b, b - 1, b + 1)
            iteration(BATCHES - 1, BATCHES - 2, None)
            iteration(None, BATCHES - 1, None)


def kernel(x, L0_tok_emb, L0_tok_W, L0_tok_b, L0_attn_W, L0_attn_a, L0_ffn_gate_w, L0_ffn_gate_b, L0_ffn_w1,
           L0_ffn_b1, L0_ffn_w2, L0_ffn_b2, L0_ffn_gamma, L0_ffn_beta):
    import numpy as np
    import concourse.bacc as bacc
    from concourse import mybir
    from concourse.bass_utils import run_bass_kernel_spmd

    batches, seq = x.shape
    tiles = seq // PARTS
    taps_w = np.asarray(L0_tok_W)
    hidden = taps_w.shape[0]
    by_tile = np.asarray(x).reshape(batches, PARTS, tiles)
    arrays = {
        "ids": by_tile.transpose(1, 0, 2).reshape(PARTS, batches * tiles),
        "id_row": by_tile.transpose(0, 2, 1).reshape(1, batches * seq),
        "emb": np.asarray(L0_tok_emb),
        "conv_rows": taps_w.transpose(2, 1, 0).reshape(-1, hidden),
        "conv_taps": taps_w.transpose(1, 2, 0),
        "conv_b": np.asarray(L0_tok_b).reshape(1, -1),
        "att_w": np.asarray(L0_attn_W),
        "att_wt": np.asarray(L0_attn_W).T,
        "att_a": np.asarray(L0_attn_a).reshape(2, hidden).T,
        "gate_w": np.asarray(L0_ffn_gate_w),
        "gate_b": np.asarray(L0_ffn_gate_b).reshape(1, -1),
        "w1": np.asarray(L0_ffn_w1).transpose(1, 0, 2).reshape(hidden, -1),
        "b1": np.asarray(L0_ffn_b1).T,
        "w2": np.asarray(L0_ffn_w2).transpose(1, 0, 2),
        "b2": np.asarray(L0_ffn_b2).reshape(-1, 2 * hidden).T,
        "gamma": np.asarray(L0_ffn_gamma).reshape(1, -1),
        "beta": np.asarray(L0_ffn_beta).reshape(1, -1),
    }
    arrays = {name: np.ascontiguousarray(a) for name, a in arrays.items()}
    nc = bacc.Bacc("TRN2", target_bir_lowering=False, num_devices=1)
    args = {name: nc.dram_tensor(f"in_{name}", a.shape, mybir.dt.from_np(a.dtype), kind="ExternalInput").ap()
            for name, a in arrays.items()}
    out = nc.dram_tensor("out", (batches, seq, hidden), mybir.dt.float32, kind="ExternalOutput").ap()
    tower(nc, out=out, **args)
    r = run_bass_kernel_spmd(nc, [{f"in_{name}": a for name, a in arrays.items()}], core_ids=[0])
    return r.results[0]["out"]
```

```python
import concourse.bass as bass
from concourse import mybir
from contextlib import ExitStack

PARTS = 128


def tower(nc, ids, id_row, emb, conv_chunks, turned_small, dup_small, rows_bc, w1, ffn_cols, experts, out):
    f32, f32r, i32, u32 = mybir.dt.float32, mybir.dt.float32r, mybir.dt.int32, mybir.dt.uint32
    ALU, ACT, AX = mybir.AluOpType, mybir.ActivationFunctionType, mybir.AxisListType.X

    VOCAB, H = emb.shape
    TAPS = turned_small.shape[1] // H - 2
    HALF = TAPS // 2
    BATCHES, SEQ, _ = out.shape
    TILES = SEQ // PARTS
    E, F = experts, ffn_cols.shape[0]
    PAIRS = E // 2
    ADDS = PAIRS - 1
    WIN = TAPS * H
    FULL = WIN // PARTS
    REST = WIN - FULL * PARTS
    EDGE = 4 * HALF
    BIAS_ROW = REST + EDGE
    LAST = BIAS_ROW + 1
    NH = H + 2
    GROW = 32
    ALPHA, EPS = 0.01, 1e-5
    UP_SLOTS = 2
    HIDDEN_PAIRS = 2
    BC_SLOTS = 2
    SUM_SLOTS = 4

    ctx = ExitStack()
    with ctx:
        def sb(name, shape, dt=f32):
            return ctx.enter_context(nc.sbuf_tensor(name, shape, dt))

        def sem(name):
            return ctx.enter_context(nc.semaphore(name))

        ident = sb("ident", [PARTS, PARTS])
        minus_half = sb("minus_half", [PARTS, TILES])
        expert_no = sb("expert_no", [PARTS, TILES, E])
        fold = sb("fold", [PARTS, H])
        spread_no = sb("spread_no", [2 * GROW, PAIRS, PARTS])
        spread = sb("spread", [2 * GROW, PAIRS, PARTS], f32r)
        id_cols = sb("id_cols", [PARTS, BATCHES * TILES], i32)
        window_at = sb("window_at", [PARTS, BATCHES * TILES], i32)
        window_now = sb("window_now", [PARTS, TILES], i32)
        id_bc = sb("id_bc", [REST + EDGE, BATCHES * SEQ], i32)
        edge_no = sb("edge_no", [REST + EDGE, 1])
        edge_high = sb("edge_high", [REST + EDGE, 1])
        edge_id = sb("edge_id", [REST + EDGE, 1])
        NV = TAPS + 2 * HALF
        edge_rows = sb("edge_rows", [2 * TAPS, H])
        edge_rows_t = sb("edge_rows_t", [H, 2 * NV])
        edge_diff = sb("edge_diff", [H, TAPS, EDGE])
        conv_w = sb("conv_w", [PARTS, FULL + 1, H])
        conv_w_last = conv_w[:, FULL, :]
        turned_raw = sb("turned_raw", [H, 2 + (2 + TAPS) * H])
        a_cols = turned_raw[:, 0:2]
        att_wt_dup = turned_raw[:, 2:2 + 2 * H]
        taps = turned_raw[:, 2 + 2 * H:].rearrange("h (k o) -> h k o", k=TAPS)
        a_rep = sb("a_rep", [H, 2 + 2 * PARTS])
        dup_raw = sb("dup_raw", [PARTS, E + NH])
        gate_raw, wh_raw = dup_raw[:, 0:E], dup_raw[:, E:E + NH]
        wh_hi = sb("wh_hi", [PARTS, NH], f32r)
        wh_lo = sb("wh_lo", [H, NH], f32r)
        wf_hi = sb("wf_hi", [PARTS, 2, PARTS], f32r)
        wf_lo = sb("wf_lo", [H, 2, PARTS], f32r)
        gate_hi = sb("gate_hi", [PARTS, E], f32r)
        gate_lo = sb("gate_lo", [H, E], f32r)
        rows_raw = sb("rows_raw", [PARTS, E + 2 * H])
        gate_bias, gamma_bc, beta_bc = rows_raw[:, 0:E], rows_raw[:, E:E + H], rows_raw[:, E + H:]
        w1_raw = sb("w1_raw", [H, E * F])
        w1_hi = sb("w1_hi", [PARTS, E * F], f32r)
        w1_lo = sb("w1_lo", [H, E * F], f32r)
        ffn_raw = sb("ffn_raw", [PARTS, E + PAIRS + E * H])
        b1_cols, b2_cols = ffn_raw[:, 0:E], ffn_raw[:, E:E + PAIRS]
        w2_sb = ffn_raw[:, E + PAIRS:].rearrange("f (e h) -> f e h", e=E)

        win_first = sb("win_first", [PARTS, TILES, WIN])
        win = sb("win", [PARTS, TILES, WIN])
        win_t = sb("win_t", [PARTS, TILES, FULL, PARTS])
        win_t_last = sb("win_t_last", [96, SEQ])
        conv_out = sb("conv_out", [PARTS, SEQ // 2])
        h0 = sb("h0", [PARTS, TILES, H])
        z1 = sb("z1", [PARTS, TILES, H])
        z1_t = sb("z1_t", [PARTS, SEQ], f32r)
        f2_max = sb("f2_max", [PARTS, 1])
        s_min = sb("s_min", [PARTS, SEQ])
        s_max = sb("s_max", [PARTS, SEQ])
        exp_a = sb("exp_a", [PARTS, SEQ])
        exp_b = sb("exp_b", [PARTS, SEQ])
        f2_diff = sb("f2_diff", [PARTS, TILES])
        exp_r = sb("exp_r", [PARTS, TILES])
        hv = sb("hv", [PARTS, TILES, H + 1])
        probs = sb("probs", [PARTS, TILES, SEQ])
        rden = sb("rden", [PARTS, TILES])
        att = sb("att", [PARTS, TILES, H])
        att_neg = sb("att_neg", [PARTS, TILES, H])
        att_exp = sb("att_exp", [PARTS, TILES, H])
        att_res = sb("att_res", [PARTS, TILES, H])
        h1 = sb("h1", [PARTS, TILES, H])
        z2 = sb("z2", [PARTS, TILES, H])
        z2_t = sb("z2_t", [PARTS, SEQ], f32r)
        z2_up = sb("z2_up", [PARTS, SEQ], f32r)
        logits = sb("logits", [PARTS, TILES, E])
        top = sb("top", [PARTS, TILES, 8])
        top_at = sb("top_at", [PARTS, TILES, 8], u32)
        top_no = sb("top_no", [PARTS, TILES, 2])
        gap = sb("gap", [PARTS, TILES])
        gap_exp = sb("gap_exp", [PARTS, TILES])
        gap_sum = sb("gap_sum", [PARTS, TILES])
        gate_1 = sb("gate_1", [PARTS, TILES])
        gate_2 = sb("gate_2", [PARTS, TILES])
        is_1 = sb("is_1", [PARTS, TILES, E])
        is_2 = sb("is_2", [PARTS, TILES, E])
        gates = sb("gates", [PARTS, TILES, E])
        gates_t = sb("gates_t", [2 * GROW, SEQ], f32r)
        ln = [dict(stats=sb(f"ln{n}_stats", [PARTS, TILES, 6]), moments=sb(f"ln{n}_moments", [PARTS, TILES, 2]),
                   var=sb(f"ln{n}_var", [PARTS, TILES]), rstd=sb(f"ln{n}_rstd", [PARTS, TILES]))
              for n in range(3)]

        hidden = sb("hidden", [F, 2 * HIDDEN_PAIRS, SEQ])
        gate_bc = sb("gate_bc", [PARTS, BC_SLOTS, SEQ])
        scaled = sb("scaled", [PARTS, SUM_SLOTS, SEQ])
        moe = sb("moe", [PARTS, SEQ])
        z2_kept = sb("z2_kept", [PARTS, BATCHES * TILES, H])
        h1_beta = sb("h1_beta", [PARTS, BATCHES * TILES, H])
        y = sb("y", [PARTS, TILES, H])
        y_norm = sb("y_norm", [PARTS, TILES, H])
        y_gam = sb("y_gam", [PARTS, TILES, H])
        y_out = sb("y_out", [PARTS, TILES, H])

        bank = [ctx.enter_context(nc.psum_tensor(f"bank{n}", [PARTS, 512], f32)) for n in range(8)]
        ps_a, ps_b, ps_small, ps_wide = bank[0], bank[1], bank[2], bank[7]
        ps_up = bank[3:5]
        ps_down, ps_bc = bank[5], bank[6]
        turn_banks, first_turn_banks = (ps_b, ps_a, ps_wide), (ps_up[0], ps_up[1], ps_down)
        turned_h = ps_small[:, 256:512].rearrange("p (t a h) -> p a t h", t=2, a=2)
        small_nh = ps_small[:, 0:TILES * NH].rearrange("p (q h) -> p q h", q=TILES)
        att_ps = ps_a[:, 0:TILES * (H + 1)].rearrange("p (q h) -> p q h", q=TILES)
        folded = ps_down[:, 0:TILES * H].rearrange("p (q h) -> p q h", q=TILES)
        last_folded = ps_wide[:, 0:TILES * H].rearrange("p (q h) -> p q h", q=TILES)

        ids_in, rows_in, edge_in, conv_in, turned_in, dup_in, bc_in, w1_in, ffn_in = [
            sem(n) for n in ("ids_in", "rows_in", "edge_in", "conv_in", "turned_in", "dup_in", "bc_in", "w1_in", "ffn_in")]
        const_made, ident_made, windows_known, edge_known = [
            sem(n) for n in ("const_made", "ident_made", "windows_known", "edge_known")]
        window_copied = sem("window_copied")
        setup_chain = sem("setup_chain")
        edge_rows_ps, edge_rows_sb, edge_diff_sb, edge_ps, conv_w_made = [
            sem(n) for n in ("edge_rows_ps", "edge_rows_sb", "edge_diff_sb", "edge_ps", "conv_w_made")]
        a_rep_made, wa_ps, wa_hi_made, wa_made, gate_hi_made, gate_made, w1_hi_made, w1_made = [
            sem(n) for n in ("a_rep_made", "wa_ps", "wa_hi_made", "wa_made", "gate_hi_made", "gate_made",
                             "w1_hi_made", "w1_made")]
        gathered_first = [sem(f"gathered_first{q}") for q in range(TILES)]
        gathered = [sem(f"gathered{q}") for q in range(TILES)]
        win_t_ps, win_t_act, win_t_dve, win_t_rest, edge_hot, conv_ps = [
            sem(n) for n in ("win_t_ps", "win_t_act", "win_t_dve", "win_t_rest", "edge_hot", "conv_ps")]
        h0_saved, z1_made, z1_t_ps, z1_hi_made, z1_t_made, f2_ps, f1_ps, h_ps = [
            sem(n) for n in ("h0_saved", "z1_made", "z1_t_ps", "z1_hi_made", "z1_t_made", "f2_ps", "f1_ps",
                             "h_ps")]
        s_min_made, s_max_made, f2_diff_made, exp_a_made, exp_b_made, exp_r_made, exp_v_made = [
            sem(n) for n in ("s_min_made", "s_max_made", "f2_diff_made", "exp_a_made", "exp_b_made",
                             "exp_r_made", "exp_v_made")]
        probs_made, hv_made, att_done, att_made, att_neg_made, att_exp_made, h1_made, h1_beta_made = [
            sem(n) for n in ("probs_made", "hv_made", "att_done", "att_made", "att_neg_made", "att_exp_made", "h1_made",
                             "h1_beta_made")]
        z2_made, z2_t_ps, z2_hi_made, z2_t_made, logits_ps, gap_made, gap_exp_made, gates_made = [
            sem(n) for n in ("z2_made", "z2_t_ps", "z2_hi_made", "z2_t_made", "logits_ps", "gap_made",
                             "gap_exp_made", "gates_made")]
        stats_made = [sem(f"stats_made{n}") for n in range(3)]
        var_made = [sem(f"var_made{n}") for n in range(3)]
        rstd_made = [sem(f"rstd_made{n}") for n in range(3)]
        gates_t_ps, gates_hi_made, gates_t_made, z2_kept_made, conv_out_made, turned_ps = [
            sem(n) for n in ("gates_t_ps", "gates_hi_made", "gates_t_made", "z2_kept_made", "conv_out_made", "turned_ps")]
        up_ps, hidden_made, down_ps, bc_ps, bc_made, scaled_made, moe_added, fold_ps, y_made, out_made, out_stored = [
            sem(n) for n in ("up_ps", "hidden_made", "down_ps", "bc_ps", "bc_made", "scaled_made", "moe_added",
                             "fold_ps", "y_made", "out_made", "out_stored")]
        logits_made, spread_made, z2_up_made = sem("logits_made"), sem("spread_made"), sem("z2_up_made")
        z1_first_made, y_used, out_chain, last_chain = sem("z1_first_made"), sem("y_used"), sem("out_chain"), sem("last_chain")
        front_chain, norm_chain, ffn_chain = sem("front_chain"), sem("norm_chain"), sem("ffn_chain")

        block = ctx.enter_context(nc.Block())

        def tiles(t, b):
            return t[:, bass.ds(b * TILES, TILES), :]

        def over_h(t, n=H):
            return t.unsqueeze(2).to_broadcast([PARTS, TILES, n])

        def write_y(eng, b, chain, chain_before):
            eng.wait_ge(windows_known, 2)
            eng.wait_ge(rstd_made[2], b + 1)
            for q in range(TILES):
                last = eng.tensor_scalar(y_norm[:, q, :], y[:, q, :], ln[2]["moments"][:, q, 0:1],
                                         ln[2]["rstd"][:, q:q + 1], ALU.subtract, ALU.mult)
            last.then_inc(y_used, 1)
            eng.wait_ge(y_used, b + 2)
            eng.tensor_tensor(y_gam[:, :, :], y_norm[:, :, :], gamma_bc.unsqueeze(1).to_broadcast([PARTS, TILES, H]),
                              ALU.mult).then_inc(chain, 1)
            eng.wait_ge(chain, chain_before + 1)
            eng.wait_ge(h1_beta_made, b + 1)
            eng.wait_ge(out_stored, 16 * b + 1)
            eng.tensor_tensor(y_out[:, :, :], y_gam[:, :, :], tiles(h1_beta, b), ALU.add).then_inc(out_made, 1)

        @block.sync
        def _(sp):
            sp.dma_start(id_cols[:, :], ids).then_inc(ids_in, 16)
            sp.dma_start(id_bc[REST:REST + EDGE, :], id_row.to_broadcast([EDGE, BATCHES * SEQ])).then_inc(rows_in, 16)
            sp.dma_start(conv_w[:, :, :].rearrange("p c o -> p (c o)"), conv_chunks).then_inc(conv_in, 16)
            sp.wait_ge(gathered_first[TILES - 1], 16)
            sp.dma_start(rows_raw[:, :], rows_bc.to_broadcast([PARTS, E + 2 * H])).then_inc(bc_in, 16)
            sp.dma_start(w1_raw[:, :], w1).then_inc(w1_in, 16)
            sp.dma_start(ffn_raw[:, :], ffn_cols).then_inc(ffn_in, 16)
            sp.sem_inc(out_stored, 1)
            with sp.Fori(0, BATCHES) as b:
                sp.wait_ge(out_made, b + 1)
                sp.dma_start(out[bass.ds(b, 1), :, :].rearrange("a (p q) h -> p (a q h)", q=TILES),
                             y_out[:, :, :].rearrange("p q h -> p (q h)")).then_inc(out_stored, 16)
            sp.wait_ge(out_stored, 16 * BATCHES + 1)

        @block.gpsimd
        def _(pool):
            pool.memset(ident[:, :], 0.0).then_inc(ident_made, 1)
            pool.memset(minus_half[:, :], -0.5).then_inc(const_made, 1)
            pool.wait_ge(ident_made, 1)
            pool.affine_select(out=ident[:, :], in_=ident[:, :], compare_op=ALU.not_equal, fill=1.0, base=0,
                               pattern=[[-1, PARTS]], channel_multiplier=1).then_inc(ident_made, 1)
            pool.wait_ge(ident_made, 2)
            pool.iota(edge_no[REST:REST + EDGE, :], pattern=[[0, 1]], base=0, channel_multiplier=1,
                      allow_small_or_imprecise_dtypes=True).then_inc(const_made, 1)

            def gather(b, dst, arrived):
                for q in range(TILES):
                    pool.indirect_dma_start(dst[:, q, :], None, emb,
                                            bass.IndirectOffsetOnAxis(ap=window_at[:, b * TILES + q:b * TILES + q + 1], axis=0)
                                            ).then_inc(arrived[q], 16)

            def gather_next(b, tiles_now):
                for q in tiles_now:
                    pool.wait_ge(windows_known, 2)
                    pool.wait_ge(win_t_ps, b * TILES + q + 1)
                    pool.tensor_copy(window_now[:, q:q + 1], window_at[:, bass.ds((b + 1) * TILES + q, 1)]).then_inc(window_copied, 1)
                    pool.wait_ge(windows_known, 2)
                    pool.wait_ge(window_copied, (b - 1) * TILES + q + 1)
                    pool.indirect_dma_start(win[:, q, :], None, emb,
                                            bass.IndirectOffsetOnAxis(ap=window_now[:, q:q + 1], axis=0)
                                            ).then_inc(gathered[q], 16)

            def inverse_deviation(n, b):
                pool.wait_ge(var_made[n], b + 1)
                pool.tensor_tensor(ln[n]["rstd"][:, :], ln[n]["var"][:, :], minus_half[:, :], ALU.pow).then_inc(rstd_made[n], 1)

            def add_pair(b, pair):
                pool.wait_ge(scaled_made, b * PAIRS + pair + 1 + BC_SLOTS)
                now = scaled[:, pair % SUM_SLOTS, :]
                if pair == 1:
                    pool.wait_ge(fold_ps, b + 1)
                    pool.tensor_tensor(moe[:, :], scaled[:, 0, :], now, ALU.add).then_inc(moe_added, 1)
                else:
                    pool.wait_ge(moe_added, b * ADDS + pair)
                    pool.tensor_tensor(moe[:, :], moe[:, :], now, ALU.add).then_inc(moe_added, 1)

            def add_beta(b):
                pool.wait_ge(h1_made, b + 1)
                pool.tensor_tensor(tiles(h1_beta, b), h1[:, :, :],
                                   beta_bc.unsqueeze(1).to_broadcast([PARTS, TILES, H]), ALU.add).then_inc(h1_beta_made, 1)

            def iteration(front, ffn, ahead, gather_more):
                if ffn is not None:
                    add_pair(ffn, 1)
                if front is not None:
                    inverse_deviation(1, front)
                if ffn is not None:
                    add_pair(ffn, 2)
                if gather_more:
                    gather_next(ahead + 1, range(0, TILES // 2))
                if ffn is not None:
                    add_pair(ffn, 3)
                if ahead is not None:
                    inverse_deviation(0, ahead)
                if gather_more:
                    gather_next(ahead + 1, range(TILES // 2, TILES))
                if ffn is not None:
                    add_pair(ffn, 4)
                if front is not None:
                    add_beta(front)
                if ffn is not None:
                    add_pair(ffn, 5)
                    add_pair(ffn, 6)
                    if front is not None:
                        add_pair(ffn, 7)
                    inverse_deviation(2, ffn)
                    if front is not None:
                        write_y(nc.gpsimd, ffn, out_chain, ffn)

            pool.wait_ge(windows_known, 2)
            gather(0, win_first, gathered_first)
            gather(1, win, gathered)
            pool.wait_ge(const_made, 2)
            inverse_deviation(0, 0)
            pool.wait_ge(rstd_made[0], 1)
            pool.iota(spread_no[0:GROW, :, :], pattern=[[2, PAIRS], [1, 2], [0, H]], base=0, channel_multiplier=-1,
                      allow_small_or_imprecise_dtypes=True).then_inc(const_made, 1)
            pool.iota(spread_no[GROW:2 * GROW, :, :], pattern=[[2, PAIRS], [1, 2], [0, H]], base=0, channel_multiplier=-1,
                      allow_small_or_imprecise_dtypes=True).then_inc(const_made, 1)
            pool.wait_ge(const_made, 4)
            gather_next(1, range(TILES))
            pool.wait_ge(bc_in, 16)
            pool.sem_inc(moe_added, 1)
            pool.sem_inc(y_used, 1)
            iteration(0, None, 1, True)
            if BATCHES > 4:
                with pool.Fori(1, BATCHES - 3) as b:
                    iteration(b, b - 1, b + 1, True)
            with pool.Fori(BATCHES - 3, BATCHES - 1) as b:
                iteration(b, b - 1, b + 1, False)
            iteration(BATCHES - 1, BATCHES - 2, None, False)
            iteration(None, BATCHES - 1, None, False)

        @block.scalar
        def _(act):
            act.dma_start(edge_rows[0:TAPS, :], emb[0:TAPS, :]).then_inc(edge_in, 16)
            act.dma_start(edge_rows[TAPS:2 * TAPS, :], emb[VOCAB - TAPS:VOCAB, :]).then_inc(edge_in, 16)
            act.dma_start(turned_raw[:, :], turned_small).then_inc(turned_in, 16)
            act.dma_start(dup_raw[:, 0:E + H], dup_small).then_inc(dup_in, 16)

            act.wait_ge(edge_rows_ps, 1)
            act.activation(edge_rows_t[:, 0:2 * HALF], ps_up[0][0:H, 0:1].to_broadcast([H, 2 * HALF]), ACT.Copy).then_inc(edge_rows_sb, 1)
            act.activation(edge_rows_t[:, 2 * HALF:NV + TAPS], ps_up[0][0:H, 0:2 * TAPS], ACT.Copy).then_inc(edge_rows_sb, 1)
            act.activation(edge_rows_t[:, NV + TAPS:2 * NV], ps_up[0][0:H, 2 * TAPS - 1:2 * TAPS].to_broadcast([H, 2 * HALF]),
                           ACT.Copy).then_inc(edge_rows_sb, 1)

            def round_small_weights():
                act.wait_ge(wa_ps, 1)
                act.activation(wh_raw[:, H:NH], ps_wide[:, 0:2], ACT.Copy).then_inc(wa_hi_made, 1)
                act.activation(wf_hi[:, :, :].rearrange("p a b -> p (a b)"), ps_wide[:, 2:2 + 2 * PARTS], ACT.Copy).then_inc(wa_hi_made, 1)
                act.wait_ge(dup_in, 16)
                act.wait_ge(wa_hi_made, 2)
                act.activation(wh_hi[:, :], wh_raw, ACT.Copy).then_inc(wa_hi_made, 1)
                act.activation(gate_hi[:, :], gate_raw, ACT.Copy).then_inc(gate_hi_made, 1)

            def copy_windows(b, q, banks=turn_banks):
                act.wait_ge(win_t_ps, b * TILES + q + 1)
                act.activation(win_t[:, q, :, :].rearrange("p c t -> p (c t)"), banks[q % 2][:, :], ACT.Copy).then_inc(win_t_act, 1)

            def copy_last_rows(b, banks=turn_banks):
                act.wait_ge(win_t_ps, b * TILES + TILES)
                act.activation(win_t_last[0:REST, :], banks[2][0:REST, :], ACT.Copy).then_inc(win_t_rest, 1)

            def copy_convolution(b, src=ps_small):
                act.wait_ge(conv_ps, b + 1)
                act.activation(conv_out[:, :], src[:, 0:SEQ // 2], ACT.Copy).then_inc(conv_out_made, 1)

            def save_h0(b, first=False):
                act.wait_ge(turned_ps, b + 1)
                if not first:
                    act.wait_ge(h1_made, b)
                act.activation(h0[:, :, :].rearrange("p (a t) h -> p a t h", a=2), turned_h, ACT.Copy).then_inc(h0_saved, 1)

            def round_z1(b):
                act.wait_ge(z1_t_ps, b + 1)
                act.activation(z1_t[0:H, :], ps_a[0:H, :], ACT.Copy).then_inc(z1_hi_made, 1)

            def exps(b):
                act.wait_ge(s_min_made, b + 1)
                act.activation(exp_a[:, :], s_min[:, :], ACT.Exp, scale=1.0 - ALPHA).then_inc(exp_a_made, 1)
                act.wait_ge(f2_diff_made, b + 1)
                act.activation(exp_r[:, :], f2_diff[:, :], ACT.Exp, scale=1.0 - ALPHA).then_inc(exp_r_made, 1)
                act.activation(hv[:, :, H:H + 1], f2_diff[:, :].unsqueeze(2), ACT.Exp, scale=ALPHA).then_inc(exp_v_made, 1)
                act.wait_ge(s_max_made, b + 1)
                act.activation(exp_b[:, :], s_max[:, :], ACT.Exp, scale=-(1.0 - ALPHA)).then_inc(exp_b_made, 1)

            def exp_negative_part(b):
                act.wait_ge(att_neg_made, b + 1)
                act.activation(att_exp[:, :, :], att_neg[:, :, :], ACT.Exp).then_inc(att_exp_made, 1)

            def round_z2(b):
                act.wait_ge(z2_t_ps, b + 1)
                act.activation(z2_t[0:H, :], ps_small[0:H, :], ACT.Copy).then_inc(z2_hi_made, 1)

            def keep_z2(b):
                act.wait_ge(z2_t_made, b + 1)
                act.activation(z2_up[:, :], z2_t[:, :].bitcast(f32), ACT.Copy).then_inc(z2_up_made, 1)
                act.activation(tiles(z2_kept, b), z2[:, :, :], ACT.Copy).then_inc(z2_kept_made, 1)

            def exp_gap(b):
                act.wait_ge(gap_made, b + 1)
                act.activation(gap_exp[:, :], gap[:, :], ACT.Exp).then_inc(gap_exp_made, 1)

            def round_gates(b):
                act.wait_ge(gates_t_ps, b + 1)
                act.activation(gates_t[0:E, :], ps_bc[0:E, :], ACT.Copy).then_inc(gates_hi_made, 1)

            def hide(b, pair, which=(0, 1)):
                for e in [2 * pair + a for a in which]:
                    act.wait_ge(up_ps, b * E + e + 1)
                    act.wait_ge(down_ps, b * PAIRS + pair + 1)
                    act.activation(hidden[:, e % (2 * HIDDEN_PAIRS), :], ps_up[e % UP_SLOTS][:, :], ACT.Relu,
                                   bias=b1_cols[:, e:e + 1]).then_inc(hidden_made, 1)

            def copy_gates(b, pair):
                act.wait_ge(bc_ps, b * PAIRS + pair + 1)
                act.wait_ge(scaled_made, b * PAIRS + pair + 1)
                act.activation(gate_bc[:, pair % BC_SLOTS, :], ps_bc[:, :], ACT.Copy).then_inc(bc_made, 1)

            def step(b, pair):
                if b is None:
                    return
                copy_gates(b, pair)
                if pair + 1 < PAIRS:
                    hide(b, pair + 1)

            def round_w1(copy):
                act.wait_ge(w1_in, 16)
                act.activation(w1_hi[copy * H:(copy + 1) * H, :], w1_raw[:, :], ACT.Copy).then_inc(w1_hi_made, 1)

            def turn_windows(b):
                copy_windows(b, 0)
                copy_windows(b, 2)
                copy_last_rows(b)

            def iteration(front, ffn, ahead, turn, first=False):
                if ffn is not None:
                    hide(ffn, 1)
                    copy_gates(ffn, 0)
                if front is not None:
                    exps(front)
                if first:
                    copy_convolution(ahead, ps_bc)
                    round_w1(1)
                step(ffn, 1)
                if front is not None:
                    exp_negative_part(front)
                step(ffn, 2)
                if first:
                    copy_windows(turn, 0, first_turn_banks)
                    copy_windows(turn, 2, first_turn_banks)
                if ahead is not None:
                    save_h0(ahead)
                if turn is not None and not first:
                    copy_windows(turn, 0)
                step(ffn, 3)
                if turn is not None and not first:
                    copy_windows(turn, 2)
                if turn is not None:
                    copy_last_rows(turn, first_turn_banks if first else turn_banks)
                step(ffn, 4)
                if front is not None:
                    round_z2(front)
                if first:
                    copy_convolution(turn, ps_bc)
                step(ffn, 5)
                if front is not None and turn is not None:
                    exp_gap(front)
                if turn is not None and not first:
                    copy_convolution(turn)
                step(ffn, 6)
                if front is not None and turn is None:
                    exp_gap(front)
                if front is not None:
                    keep_z2(front)
                step(ffn, 7)
                if ahead is not None:
                    round_z1(ahead)
                if front is not None:
                    hide(front, 0)
                    round_gates(front)

            turn_windows(0)
            copy_convolution(0)
            save_h0(0, first=True)
            round_small_weights()
            copy_windows(1, 0, first_turn_banks)
            copy_windows(1, 2, first_turn_banks)
            round_z1(0)
            copy_last_rows(1, first_turn_banks)
            round_w1(0)
            act.sem_inc(hidden_made, UP_SLOTS)
            act.sem_inc(bc_made, 1)
            act.wait_ge(ffn_in, 16)
            iteration(0, None, 1, 2, first=True)
            with act.Fori(1, BATCHES - 2) as b:
                iteration(b, b - 1, b + 1, b + 2)
            iteration(BATCHES - 2, BATCHES - 3, BATCHES - 1, None)
            iteration(BATCHES - 1, BATCHES - 2, None, None)
            iteration(None, BATCHES - 1, None, None)

        @block.tensor
        def _(pe):
            def split_matmul(dst, lhs, lhs_lo, rhs, rhs_lo):
                nc.tensor.matmul(dst, lhs, rhs, start=True, stop=False)
                return nc.tensor.matmul(dst, lhs_lo, rhs_lo, start=False, stop=True)

            pe.sem_inc(down_ps, HIDDEN_PAIRS)
            pe.sem_inc(fold_ps, 1)
            pe.wait_ge(ident_made, 2)

            def keep_clock(products):
                for _ in range(products):
                    nc.tensor.matmul(ps_bc[:, 0:PARTS], ident[:, :], ident[:, :], start=True, stop=True)

            keep_clock(6)
            pe.wait_ge(edge_in, 16 * 2)
            nc.tensor.transpose(ps_up[0][0:H, 0:2 * TAPS], edge_rows[:, :], ident[0:2 * TAPS, 0:2 * TAPS]).then_inc(edge_rows_ps, 1)
            keep_clock(5)

            def weigh_edges():
                pe.wait_ge(turned_in, 16)
                pe.wait_ge(edge_diff_sb, 1)
                for k in range(TAPS):
                    last = nc.tensor.matmul(ps_up[1][REST:REST + EDGE, 0:H], edge_diff[:, k, :], taps[:, k, :],
                                            start=(k == 0), stop=(k == TAPS - 1))
                last.then_inc(edge_ps, 1)

            def weigh_scores():
                pe.wait_ge(a_rep_made, 3)
                nc.tensor.matmul(ps_wide[:, 0:2 + 2 * PARTS], att_wt_dup, a_rep[:, :], start=True, stop=True).then_inc(wa_ps, 1)

            def turn_tile(q, source, banks):
                for c in range(FULL):
                    nc.tensor.transpose(banks[q % 2][:, c * PARTS:(c + 1) * PARTS],
                                        source[:, q, c * PARTS:(c + 1) * PARTS], ident[:, :])
                nc.tensor.transpose(banks[2][0:REST, q * PARTS:(q + 1) * PARTS],
                                    source[:, q, FULL * PARTS:WIN], ident[:, :]).then_inc(win_t_ps, 1)

            def turn_windows(b, tiles_now, banks=turn_banks):
                for q in tiles_now:
                    pe.wait_ge(gathered[q], 16 * b)
                    if q == 0 and banks is turn_banks:
                        pe.wait_ge(s_max_made, b - 1)
                    elif q == 1 and banks is turn_banks:
                        pe.wait_ge(att_made, b - 1)
                    elif q == 2:
                        pe.wait_ge(win_t_act, 2 * b + 1)
                    elif q == 3:
                        pe.wait_ge(win_t_dve, 2 * b + 1)
                    turn_tile(q, win, banks)

            def convolve(b, dst=ps_small):
                pe.wait_ge(win_t_act, 2 * b + 2)
                pe.wait_ge(win_t_dve, 2 * b + 2)
                pe.wait_ge(win_t_rest, b + 1)
                pe.wait_ge(edge_hot, b + 1)
                weights = [conv_w[:, c, :] for c in range(FULL)] + [conv_w_last[0:LAST, :]]
                for c, w in enumerate(weights):
                    for a in range(2):
                        if c < FULL:
                            windows = win_t[:, 2 * a:2 * a + 2, c, :]
                        else:
                            windows = win_t_last[0:LAST, a * SEQ // 2:(a + 1) * SEQ // 2]
                        last = nc.tensor.matmul(dst[a * H:(a + 1) * H, 0:SEQ // 2], w, windows,
                                                start=(c == 0), stop=(c == FULL))
                last.then_inc(conv_ps, 1)

            def turn_convolution(b):
                pe.wait_ge(conv_out_made, b + 1)
                for t in range(2):
                    last = nc.tensor.transpose(ps_small[:, SEQ // 2 + t * PARTS:SEQ // 2 + (t + 1) * PARTS],
                                               conv_out[:, t * PARTS:(t + 1) * PARTS], ident[:, :])
                last.then_inc(turned_ps, 1)

            def turn_z1(arrived, count):
                pe.wait_ge(ident_made, 2)
                pe.wait_ge(arrived, count)
                for q in range(TILES):
                    last = nc.tensor.transpose(ps_a[0:H, q * PARTS:(q + 1) * PARTS], z1[:, q, :], ident[:, :])
                last.then_inc(z1_t_ps, 1)

            def project(b, ahead):
                pe.wait_ge(z1_t_made, b + 1)
                split_matmul(ps_wide[:, :], wf_hi[:, 1, :], wf_lo[:, 1, :], z1_t[:, :], z1_t[0:H, :]).then_inc(f2_ps, 1)
                split_matmul(ps_b[:, :], wf_hi[:, 0, :], wf_lo[:, 0, :], z1_t[:, :], z1_t[0:H, :]).then_inc(f1_ps, 1)
                if ahead is not None:
                    pe.wait_ge(h0_saved, b + 1)
                    if not (isinstance(b, int) and b == 0):
                        pe.wait_ge(conv_out_made, b + 2)
                for q in range(TILES):
                    cols = slice(q * PARTS, (q + 1) * PARTS)
                    last = split_matmul(small_nh[:, q, :], z1_t[:, cols], z1_t[0:H, cols], wh_hi[:, :], wh_lo[:, :])
                last.then_inc(h_ps, 1)

            def attend(b):
                pe.wait_ge(hv_made, b + 1)
                for j in range(TILES):
                    pe.wait_ge(probs_made, b * TILES + j + 1)
                    for i in range(TILES):
                        last = nc.tensor.matmul(att_ps[:, i, :], probs[:, j, i * PARTS:(i + 1) * PARTS], hv[:, j, :],
                                                start=(i == 0 and j == 0), stop=(i == TILES - 1 and j == TILES - 1),
                                                skip_group_check=True)
                last.then_inc(att_done, 1)

            def turn_z2(b, ahead):
                pe.wait_ge(ident_made, 2)
                pe.wait_ge(z2_made, b + 1)
                if ahead is not None:
                    pe.wait_ge(h0_saved, b + 2)
                for q in range(TILES):
                    last = nc.tensor.transpose(ps_small[0:H, q * PARTS:(q + 1) * PARTS], z2[:, q, :], ident[:, :])
                last.then_inc(z2_t_ps, 1)

            def gate(b):
                pe.wait_ge(z2_t_made, b + 1)
                for q in range(TILES):
                    cols = slice(q * PARTS, (q + 1) * PARTS)
                    last = split_matmul(ps_wide[:, q * E:(q + 1) * E], z2_t[:, cols], z2_t[0:H, cols], gate_hi[:, :], gate_lo[:, :])
                last.then_inc(logits_ps, 1)

            def turn_gates(b, ffn):
                pe.wait_ge(gates_made, b + 1)
                if ffn is not None:
                    pe.wait_ge(bc_made, (ffn + 1) * PAIRS + 1)
                for q in range(TILES):
                    last = nc.tensor.transpose(ps_bc[0:E, q * PARTS:(q + 1) * PARTS], gates[:, q, :], ident[:, :])
                last.then_inc(gates_t_ps, 1)

            def up(b, pair, which=(0, 1)):
                if pair == 0:
                    pe.wait_ge(z2_up_made, b + 1)
                for e in [2 * pair + a for a in which]:
                    pe.wait_ge(hidden_made, b * E + e + 1)
                    split_matmul(ps_up[e % UP_SLOTS][:, :], w1_hi[:, e * F:(e + 1) * F], w1_lo[:, e * F:(e + 1) * F],
                                 z2_up[:, :], z2_up[0:H, :]).then_inc(up_ps, 1)

            def broadcast_gates(b, pair):
                if pair == 0:
                    pe.wait_ge(gates_t_made, b + 1)
                pe.wait_ge(bc_made, b * PAIRS + pair + 1)
                nc.tensor.matmul(ps_bc[:, :], spread[:, pair, :], gates_t[:, :], start=True, stop=True).then_inc(bc_ps, 1)

            def down(b, pair):
                if pair == 0:
                    pe.wait_ge(y_made, b + 1)
                else:
                    pe.wait_ge(scaled_made, b * PAIRS + pair + BC_SLOTS)
                pe.wait_ge(hidden_made, b * E + 2 * pair + 2 + UP_SLOTS)
                for a in range(2):
                    e = 2 * pair + a
                    last = nc.tensor.matmul(ps_down[a * H:(a + 1) * H, :], w2_sb[:, e, :], hidden[:, e % (2 * HIDDEN_PAIRS), :],
                                            start=True, stop=True)
                last.then_inc(down_ps, 1)

            def step(b, pair):
                if b is None:
                    return
                broadcast_gates(b, pair)
                if pair + 1 < PAIRS:
                    up(b, pair + 1)
                down(b, pair)

            def fold_last(b):
                pe.wait_ge(moe_added, b * ADDS + ADDS)
                for q in range(TILES):
                    nc.tensor.matmul(last_folded[:, q, :], moe[:, q * PARTS:(q + 1) * PARTS], fold[:, :], start=(q == 0), stop=False,
                                     skip_group_check=True)
                pe.wait_ge(scaled_made, b * PAIRS + PAIRS + BC_SLOTS)
                for q in range(TILES):
                    last = nc.tensor.matmul(last_folded[:, q, :], scaled[:, (PAIRS - 1) % SUM_SLOTS, q * PARTS:(q + 1) * PARTS], fold[:, :],
                                            start=False, stop=(q == TILES - 1), skip_group_check=True)
                last.then_inc(fold_ps, 1)

            def fold_experts(b):
                pe.wait_ge(moe_added, b * ADDS + ADDS + 1)
                for q in range(TILES):
                    last = nc.tensor.matmul(folded[:, q, :], moe[:, q * PARTS:(q + 1) * PARTS], fold[:, :], start=True, stop=True)
                last.then_inc(fold_ps, 1)

            def iteration(front, ffn, ahead, turn, first=False):
                if front is not None:
                    project(front, ahead)
                if ffn is not None:
                    up(ffn, 1, (1,))
                if ffn is not None:
                    broadcast_gates(ffn, 0)
                    down(ffn, 0)
                step(ffn, 1)
                if first:
                    convolve(ahead, ps_bc)
                if front is not None:
                    attend(front)
                step(ffn, 2)
                if ahead is not None:
                    turn_convolution(ahead)
                if first:
                    turn_windows(turn, range(0, 3), first_turn_banks)
                    keep_clock(6)
                    turn_windows(turn, range(3, TILES), first_turn_banks)
                    turn_z2(front, ahead)
                    convolve(turn, ps_bc)
                    gate(front)
                else:
                    if turn is not None:
                        turn_windows(turn, range(0, TILES // 2))
                    step(ffn, 3)
                    if turn is not None:
                        turn_windows(turn, range(TILES // 2, TILES))
                    step(ffn, 4)
                    if front is not None:
                        turn_z2(front, ahead)
                    step(ffn, 5)
                    if front is not None:
                        gate(front)
                if turn is not None and not first:
                    convolve(turn)
                step(ffn, 6)
                if ffn is not None:
                    broadcast_gates(ffn, 7)
                if ahead is not None:
                    turn_z1(z1_made, ahead)
                if ffn is not None:
                    down(ffn, 7)
                if front is not None:
                    if first:
                        pe.wait_ge(conv_out_made, 3)
                        keep_clock(8)
                        pe.wait_ge(w1_hi_made, 2)
                        pe.wait_ge(w1_made, 1)
                    up(front, 0)
                    turn_gates(front, ffn)
                    up(front, 1, (0,))
                if front is None:
                    fold_last(ffn)
                elif ffn is not None:
                    fold_experts(ffn)

            for q in range(TILES):
                pe.wait_ge(gathered_first[q], 16)
                if q == 2:
                    pe.wait_ge(win_t_act, 1)
                elif q == 3:
                    pe.wait_ge(win_t_dve, 1)
                turn_tile(q, win_first, turn_banks)
                if q < TILES - 2:
                    keep_clock(1)
                elif q == TILES - 2:
                    weigh_edges()
            keep_clock(2)
            pe.wait_ge(conv_in, 16)
            pe.wait_ge(conv_w_made, 1)
            convolve(0)
            weigh_scores()
            turn_convolution(0)
            turn_windows(1, range(0, 3), first_turn_banks)
            keep_clock(4)
            turn_z1(z1_first_made, 1)
            turn_windows(1, range(3, TILES), first_turn_banks)
            keep_clock(3)
            pe.wait_ge(wa_hi_made, 3)
            pe.wait_ge(wa_made, 2)
            pe.wait_ge(gate_hi_made, 1)
            pe.wait_ge(gate_made, 1)
            iteration(0, None, 1, 2, first=True)
            pe.wait_ge(ffn_in, 16)
            pe.wait_ge(spread_made, 2)
            with pe.Fori(1, BATCHES - 2) as b:
                iteration(b, b - 1, b + 1, b + 2)
            iteration(BATCHES - 2, BATCHES - 3, BATCHES - 1, None)
            iteration(BATCHES - 1, BATCHES - 2, None, None)
            iteration(None, BATCHES - 1, None, None)

        @block.vector
        def _(dve):
            done = [0]

            def linked(ins):
                done[0] += 1
                ins.then_inc(setup_chain, 1)
                dve.wait_ge(setup_chain, done[0])

            dve.wait_ge(ids_in, 16)
            linked(nc.vector.tensor_scalar(window_at[:, :], id_cols[:, :], float(HALF), 0.0, ALU.subtract, ALU.max))
            nc.vector.tensor_scalar(window_at[:, :], window_at[:, :], float(VOCAB - TAPS), None, ALU.min).then_inc(windows_known, 2)
            nc.vector.memset(win_t_last[REST:96, :], 1.0).then_inc(setup_chain, 1)
            done[0] += 1
            dve.wait_ge(const_made, 2)
            edge = slice(REST, REST + EDGE)
            linked(nc.vector.tensor_scalar(edge_high[edge, :], edge_no[edge, :], 2.0 * HALF - 0.5, float(VOCAB - 2 * HALF),
                                           ALU.is_gt, ALU.mult))
            linked(nc.vector.scalar_tensor_tensor(edge_id[edge, :], edge_no[edge, :], float(-HALF), edge_high[edge, :], ALU.add, ALU.add))
            dve.wait_ge(rows_in, 16)
            linked(nc.vector.tensor_scalar(id_bc[edge, :], id_bc[edge, :], float(-HALF), float(VOCAB + HALF - 1), ALU.max, ALU.min))
            dve.wait_ge(edge_rows_sb, 3)
            for k in range(TAPS):
                for end, first, base in ((0, k, 2 * HALF + k), (1, NV + 1 + k, NV + k)):
                    last = nc.vector.tensor_scalar(edge_diff[:, k, end * 2 * HALF:(end + 1) * 2 * HALF],
                                                   edge_rows_t[:, first:first + 2 * HALF], edge_rows_t[:, base:base + 1],
                                                   None, ALU.subtract)
            last.then_inc(edge_diff_sb, 1)
            def small_constants():
                dve.wait_ge(turned_in, 16)
                nc.vector.tensor_copy(a_rep[:, 0:2], a_cols[:, 1:2].to_broadcast([H, 2])).then_inc(a_rep_made, 1)
                nc.vector.tensor_copy(a_rep[:, 2:2 + PARTS], a_cols[:, 0:1].to_broadcast([H, PARTS])).then_inc(a_rep_made, 1)
                nc.vector.tensor_copy(a_rep[:, 2 + PARTS:], a_cols[:, 1:2].to_broadcast([H, PARTS])).then_inc(a_rep_made, 1)
                for e in range(E):
                    last = nc.vector.memset(expert_no[:, :, e:e + 1], float(e))
                nc.vector.memset(gates_t[:, :].bitcast(f32), 0.0)
                dve.wait_ge(ident_made, 2)
                nc.vector.tensor_copy(fold[0:H, :], ident[0:H, 0:H])
                nc.vector.tensor_copy(fold[H:2 * H, :], ident[H:2 * H, H:2 * H]).then_inc(spread_made, 1)

            def finish_edges():
                dve.wait_ge(conv_in, 16)
                dve.wait_ge(edge_ps, 1)
                nc.vector.tensor_copy(conv_w_last[edge, :], ps_up[1][edge, 0:H]).then_inc(conv_w_made, 1)

            def split_small_weights():
                dve.wait_ge(wa_hi_made, 3)
                nc.vector.tensor_tensor(wh_lo[:, :], wh_raw[0:H, :], wh_hi[0:H, :].bitcast(f32), ALU.subtract).then_inc(wa_made, 1)
                nc.vector.tensor_tensor(wf_lo[:, :, :].rearrange("p a b -> p (a b)"), ps_wide[0:H, 2:2 + 2 * PARTS],
                                        wf_hi[0:H, :, :].rearrange("p a b -> p (a b)").bitcast(f32), ALU.subtract).then_inc(wa_made, 1)
                dve.wait_ge(gate_hi_made, 1)
                nc.vector.tensor_tensor(gate_lo[:, :], gate_raw[0:H, :], gate_hi[0:H, :].bitcast(f32), ALU.subtract).then_inc(gate_made, 1)

            def split_w1():
                dve.wait_ge(w1_hi_made, 1)
                nc.vector.tensor_tensor(w1_lo[:, :], w1_raw[:, :], w1_hi[0:H, :].bitcast(f32), ALU.subtract).then_inc(w1_made, 1)

            def make_spread():
                dve.wait_ge(const_made, 4)
                nc.vector.tensor_scalar(spread[:, :, :], spread_no[:, :, :], 0.0, None, ALU.is_equal).then_inc(spread_made, 1)

            FRONT_LINKS, NORM_LINKS, FFN_LINKS = 10, 1, 1
            count = {}

            def link(ins, b, chain, per):
                count[chain] = count.get(chain, 0) + 1
                ins.then_inc(chain, 1)
                dve.wait_ge(chain, b * per + count[chain])

            def f_link(ins, b):
                link(ins, b, front_chain, FRONT_LINKS)

            def n_link(ins, b):
                link(ins, b, norm_chain, NORM_LINKS)

            def e_link(ins, b):
                link(ins, b, ffn_chain, FFN_LINKS)

            def normalise(n, b, src, linker):
                t = ln[n]
                for q in range(TILES):
                    last = nc.vector.bn_stats(t["stats"][:, q, :], src[:, q, :])
                last.then_inc(stats_made[n], 1)
                dve.wait_ge(windows_known, 2)
                dve.wait_ge(stats_made[n], b + 1)
                for q in range(TILES):
                    last = nc.vector.bn_aggr(t["moments"][:, q, :], t["stats"][:, q, :])
                linker(last, b)
                nc.vector.tensor_scalar(t["var"][:, :].unsqueeze(2), t["moments"][:, :, 1:2], EPS, None, ALU.add).then_inc(var_made[n], 1)

            def scale(n, b, dst, src):
                dve.wait_ge(rstd_made[n], b + 1)
                for q in range(TILES):
                    last = nc.vector.tensor_scalar(dst[:, q, :], src[:, q, :], ln[n]["moments"][:, q, 0:1],
                                                   ln[n]["rstd"][:, q:q + 1], ALU.subtract, ALU.mult)
                return last

            def copy_windows(b, q, banks=turn_banks):
                dve.wait_ge(win_t_ps, b * TILES + q + 1)
                nc.vector.tensor_copy(win_t[:, q, :, :].rearrange("p c t -> p (c t)"), banks[q % 2][:, :]).then_inc(win_t_dve, 1)

            def mark_edges(b, first=False):
                if not first:
                    dve.wait_ge(conv_ps, b)
                nc.vector.tensor_scalar(win_t_last[edge, :], id_bc[edge, bass.ds(b * SEQ, SEQ)], edge_id[edge, :], None,
                                        ALU.is_equal).then_inc(edge_hot, 1)

            def norm_h0(b):
                dve.wait_ge(h0_saved, b + 1)
                normalise(0, b, h0, n_link)

            def make_z1(b, arrived=z1_made):
                scale(0, b, z1, h0).then_inc(arrived, 1)

            def split_z1(b):
                dve.wait_ge(z1_hi_made, b + 1)
                nc.vector.tensor_tensor(z1_t[H:2 * H, :], ps_a[0:H, :], z1_t[0:H, :].bitcast(f32), ALU.subtract).then_inc(z1_t_made, 1)

            def scores(b):
                dve.wait_ge(f2_ps, b + 1)
                f_link(nc.vector.tensor_reduce(f2_max[:, :], ps_wide[:, :], axis=AX, op=ALU.max), b)
                dve.wait_ge(f1_ps, b + 1)
                nc.vector.tensor_scalar(s_min[:, :], ps_b[:, :], f2_max[:, :], 0.0, ALU.add, ALU.min).then_inc(s_min_made, 1)
                dve.wait_ge(h_ps, b + 1)
                nc.vector.tensor_scalar(f2_diff[:, :].unsqueeze(2), small_nh[:, :, H:H + 1], f2_max[:, :], None, ALU.subtract).then_inc(f2_diff_made, 1)
                nc.vector.tensor_scalar(s_max[:, :], ps_b[:, :], f2_max[:, :], 0.0, ALU.add, ALU.max).then_inc(s_max_made, 1)

            def make_probs(b):
                dve.wait_ge(exp_v_made, b + 1)
                nc.vector.tensor_tensor(hv[:, :, 0:H], small_nh[:, :, 0:H], hv[:, :, H:H + 1].to_broadcast([PARTS, TILES, H]),
                                        ALU.mult).then_inc(hv_made, 1)
                dve.wait_ge(exp_a_made, b + 1)
                dve.wait_ge(exp_r_made, b + 1)
                dve.wait_ge(exp_b_made, b + 1)
                for j in range(TILES):
                    nc.vector.scalar_tensor_tensor(probs[:, j, :], exp_a[:, :], exp_r[:, j:j + 1], exp_b[:, :],
                                                   ALU.mult, ALU.max).then_inc(probs_made, 1)

            def finish_attention(b):
                dve.wait_ge(att_done, b + 1)
                f_link(nc.vector.reciprocal(rden[:, :].unsqueeze(2), att_ps[:, :, H:H + 1]), b)
                nc.vector.tensor_tensor(att[:, :, :], att_ps[:, :, 0:H], over_h(rden[:, :]), ALU.mult).then_inc(att_made, 1)
                dve.wait_ge(att_made, b + 1)
                nc.vector.tensor_scalar(att_neg[:, :, :], att[:, :, :], 0.0, None, ALU.min).then_inc(att_neg_made, 1)
                dve.wait_ge(h0_saved, b + 1)
                f_link(nc.vector.scalar_tensor_tensor(att_res[:, :, :], att[:, :, :], 0.0, h0[:, :, :], ALU.max, ALU.add), b)
                dve.wait_ge(att_exp_made, b + 1)
                dve.wait_ge(h1_beta_made, b)
                nc.vector.scalar_tensor_tensor(h1[:, :, :], att_exp[:, :, :], -1.0, att_res[:, :, :], ALU.add, ALU.add).then_inc(h1_made, 1)

            def norm_h1(b):
                dve.wait_ge(h1_made, b + 1)
                normalise(1, b, h1, f_link)

            def make_z2(b):
                scale(1, b, z2, h1).then_inc(z2_made, 1)

            def split_z2(b):
                dve.wait_ge(z2_hi_made, b + 1)
                nc.vector.tensor_tensor(z2_t[H:2 * H, :], ps_small[0:H, :], z2_t[0:H, :].bitcast(f32), ALU.subtract).then_inc(z2_t_made, 1)

            def choose_experts(b):
                dve.wait_ge(logits_ps, b + 1)
                nc.vector.tensor_tensor(logits[:, :, :], ps_wide[:, 0:TILES * E].rearrange("p (q e) -> p q e", q=TILES),
                                        gate_bias.unsqueeze(1).to_broadcast([PARTS, TILES, E]), ALU.add).then_inc(logits_made, 1)
                dve.wait_ge(windows_known, 2)
                dve.wait_ge(logits_made, b + 1)
                for q in range(TILES):
                    last = nc.vector.max(top[:, q, :], logits[:, q, :])
                f_link(last, b)
                nc.vector.tensor_tensor(gap[:, :].unsqueeze(2), top[:, :, 1:2], top[:, :, 0:1], ALU.subtract).then_inc(gap_made, 1)
                for q in range(TILES):
                    last = nc.vector.max_index(top_at[:, q, :], top[:, q, :], logits[:, q, :])
                f_link(last, b)

            def weigh_experts(b):
                dve.wait_ge(gap_exp_made, b + 1)
                nc.vector.tensor_scalar(gap_sum[:, :], gap_exp[:, :], 1.0, None, ALU.add)
                f_link(nc.vector.tensor_copy(top_no[:, :, :], top_at[:, :, 0:2]), b)
                nc.vector.reciprocal(gate_1[:, :], gap_sum[:, :])
                nc.vector.tensor_tensor(is_1[:, :, :], expert_no[:, :, :], top_no[:, :, 0:1].to_broadcast([PARTS, TILES, E]), ALU.is_equal)
                f_link(nc.vector.tensor_tensor(is_2[:, :, :], expert_no[:, :, :], top_no[:, :, 1:2].to_broadcast([PARTS, TILES, E]), ALU.is_equal), b)
                nc.vector.tensor_tensor(gate_2[:, :], gap_exp[:, :], gate_1[:, :], ALU.mult)
                f_link(nc.vector.tensor_tensor(is_1[:, :, :], is_1[:, :, :], over_h(gate_1[:, :], E), ALU.mult), b)
                f_link(nc.vector.tensor_tensor(is_2[:, :, :], is_2[:, :, :], over_h(gate_2[:, :], E), ALU.mult), b)
                nc.vector.tensor_tensor(gates[:, :, :], is_1[:, :, :], is_2[:, :, :], ALU.add).then_inc(gates_made, 1)

            def split_gates(b):
                dve.wait_ge(gates_hi_made, b + 1)
                nc.vector.tensor_tensor(gates_t[GROW:GROW + E, :], ps_bc[0:E, :], gates_t[0:E, :].bitcast(f32), ALU.subtract).then_inc(gates_t_made, 1)

            def scale_pair(b, pair):
                if b is None:
                    return
                dve.wait_ge(down_ps, b * PAIRS + pair + 1 + HIDDEN_PAIRS)
                dve.wait_ge(bc_made, b * PAIRS + pair + 2)
                dve.wait_ge(moe_added, b * ADDS + 1 + (0 if pair < SUM_SLOTS else max(pair - SUM_SLOTS, 1)))
                nc.vector.scalar_tensor_tensor(scaled[:, pair % SUM_SLOTS, :], ps_down[:, :], b2_cols[:, pair:pair + 1],
                                               gate_bc[:, pair % BC_SLOTS, :], ALU.add, ALU.mult).then_inc(scaled_made, 1)

            def finish_ffn(b, sums=folded):
                dve.wait_ge(fold_ps, b + 2)
                dve.wait_ge(z2_kept_made, b + 1)
                dve.wait_ge(y_used, b + 1)
                nc.vector.tensor_tensor(y[:, :, :], sums, tiles(z2_kept, b), ALU.add).then_inc(y_made, 1)
                dve.wait_ge(y_made, b + 2)
                normalise(2, b, y, e_link)

            def iteration(front, ffn, ahead, turn, first=False):
                if front is not None:
                    scores(front)
                scale_pair(ffn, 0)
                if front is not None:
                    make_probs(front)
                if first:
                    split_w1()
                scale_pair(ffn, 1)
                if turn is not None and not first:
                    mark_edges(turn)
                if front is not None:
                    finish_attention(front)
                scale_pair(ffn, 2)
                if front is not None:
                    norm_h1(front)
                if turn is not None:
                    copy_windows(turn, 1, first_turn_banks if first else turn_banks)
                if first:
                    mark_edges(turn)
                scale_pair(ffn, 3)
                if front is not None:
                    make_z2(front)
                if turn is not None:
                    copy_windows(turn, 3, first_turn_banks if first else turn_banks)
                if ahead is not None:
                    norm_h0(ahead)
                if first:
                    make_spread()
                scale_pair(ffn, 4)
                if front is not None:
                    split_z2(front)
                if ahead is not None:
                    make_z1(ahead)
                scale_pair(ffn, 5)
                if front is not None:
                    choose_experts(front)
                if turn is None:
                    scale_pair(ffn, 6)
                if front is not None:
                    weigh_experts(front)
                if turn is not None:
                    scale_pair(ffn, 6)
                if ahead is not None:
                    split_z1(ahead)
                scale_pair(ffn, 7)
                if front is not None:
                    split_gates(front)
                if ffn is not None:
                    finish_ffn(ffn, folded if front is not None else last_folded)
                for chain, links, here in ((front_chain, FRONT_LINKS, front), (norm_chain, NORM_LINKS, ahead),
                                           (ffn_chain, FFN_LINKS, ffn)):
                    assert here is None or count.pop(chain) == links, (links, chain)
                count.clear()

            copy_windows(0, 1)
            mark_edges(0, first=True)
            finish_edges()
            copy_windows(0, 3)
            small_constants()
            norm_h0(0)
            split_small_weights()
            mark_edges(1)
            make_z1(0, z1_first_made)
            copy_windows(1, 1, first_turn_banks)
            split_z1(0)
            copy_windows(1, 3, first_turn_banks)
            count.clear()
            dve.sem_inc(scaled_made, BC_SLOTS)
            dve.sem_inc(y_made, 1)
            dve.wait_ge(bc_in, 16)
            iteration(0, None, 1, 2, first=True)
            dve.wait_ge(ffn_in, 16)
            with dve.Fori(1, BATCHES - 2) as b:
                iteration(b, b - 1, b + 1, b + 2)
            iteration(BATCHES - 2, BATCHES - 3, BATCHES - 1, None)
            iteration(BATCHES - 1, BATCHES - 2, None, None)
            iteration(None, BATCHES - 1, None, None)
            write_y(nc.vector, BATCHES - 1, last_chain, 0)


def kernel(x, L0_tok_emb, L0_tok_W, L0_tok_b, L0_attn_W, L0_attn_a, L0_ffn_gate_w, L0_ffn_gate_b, L0_ffn_w1,
           L0_ffn_b1, L0_ffn_w2, L0_ffn_b2, L0_ffn_gamma, L0_ffn_beta):
    import numpy as np
    import concourse.bacc as bacc
    from concourse import mybir
    from concourse.bass_utils import run_bass_kernel_spmd

    batches, seq = x.shape
    tiles = seq // PARTS
    taps_w = np.asarray(L0_tok_W)
    hidden = taps_w.shape[0]
    by_tile = np.asarray(x).reshape(batches, PARTS, tiles)
    experts, _, inner = np.asarray(L0_ffn_w1).shape
    taps = taps_w.shape[2]
    rows = taps * hidden
    chunks = np.zeros((-(-rows // PARTS) * PARTS, hidden), taps_w.dtype)
    chunks[:rows] = taps_w.transpose(2, 1, 0).reshape(rows, hidden)
    chunks[rows + 4 * (taps // 2)] = np.asarray(L0_tok_b)
    att_w, att_wt = np.asarray(L0_attn_W), np.asarray(L0_attn_W).T
    gate_att = np.concatenate([np.asarray(L0_ffn_gate_w), att_w], axis=1)
    arrays = {
        "ids": by_tile.transpose(1, 0, 2).reshape(PARTS, batches * tiles),
        "id_row": by_tile.transpose(0, 2, 1).reshape(1, batches * seq),
        "emb": np.asarray(L0_tok_emb),
        "conv_chunks": chunks.reshape(-1, PARTS, hidden).transpose(1, 0, 2).reshape(PARTS, -1),
        "turned_small": np.concatenate([np.asarray(L0_attn_a).reshape(2, hidden).T, att_wt, att_wt,
                                        taps_w.transpose(1, 2, 0).reshape(hidden, -1)], axis=1),
        "dup_small": np.concatenate([gate_att, gate_att], axis=0),
        "rows_bc": np.concatenate([np.asarray(v).reshape(1, -1) for v in (L0_ffn_gate_b, L0_ffn_gamma, L0_ffn_beta)], axis=1),
        "w1": np.asarray(L0_ffn_w1).transpose(1, 0, 2).reshape(hidden, -1),
        "ffn_cols": np.concatenate([np.asarray(L0_ffn_b1).T, np.asarray(L0_ffn_b2).reshape(-1, PARTS).T,
                                    np.asarray(L0_ffn_w2).transpose(1, 0, 2).reshape(inner, -1)], axis=1),
    }
    arrays = {name: np.ascontiguousarray(a) for name, a in arrays.items()}
    nc = bacc.Bacc("TRN2", target_bir_lowering=False, num_devices=1)
    args = {name: nc.dram_tensor(f"in_{name}", a.shape, mybir.dt.from_np(a.dtype), kind="ExternalInput").ap()
            for name, a in arrays.items()}
    out = nc.dram_tensor("out", (batches, seq, hidden), mybir.dt.float32, kind="ExternalOutput").ap()
    tower(nc, experts=experts, out=out, **args)
    r = run_bass_kernel_spmd(nc, [{f"in_{name}": a for name, a in arrays.items()}], core_ids=[0])
    return r.results[0]["out"]
```
